# Optimizing a Trainium2 kernel written in Bass

```python
import numpy as np
import jax
import jax.numpy as jnp

def _softmax(x, axis=-1):
    return jax.nn.softmax(x, axis=axis)
def _gelu(x):
    return jax.nn.gelu(x, approximate=True)
def _silu(x):
    return jax.nn.silu(x)
def _sigmoid(x):
    return jax.nn.sigmoid(x)
def _layernorm(x, axis=-1, eps=1e-5):
    m = jnp.mean(x, axis=axis, keepdims=True)
    v = jnp.var(x, axis=axis, keepdims=True)
    return (x - m) / jnp.sqrt(v + eps)
def _scatter_add(tgt, idx, src, axis=0):
    return tgt.at[idx].add(src)
def _segment_sum(src, seg, n):
    return jax.ops.segment_sum(src, seg, n)

kernel_name = 'mk_adj_preln_d1_adj_512_c73bf2'

def setup_inputs(seed: int = 0):
    np.random.seed(seed)
    _w = jnp.asarray
    def _rec_inputs():
        import jax
        import jax.numpy as jnp
        _gk = jax.random.key(seed)
        x = -0.0002928 + 1 * jax.random.normal(jax.random.fold_in(_gk, 1), (16, 1024, 512), jnp.float32)
        _w = (1.0 + jnp.arange(1024, dtype=jnp.float32)) ** -0.5
        _w = _w / _w.mean()
        _pij = jnp.clip(0.0078125 * _w[:, None] * _w[None, :], 0.0, 1.0)
        _a = jax.random.uniform(jax.random.fold_in(_gk, 2), (1024, 1024)) < _pij
        _a = jnp.logical_or(_a, jnp.eye(1024, dtype=bool))
        _af = _a.astype(jnp.float32)
        adj = _af
        return x, adj
    x, adj = _rec_inputs()
    def _L0_gnn_setup():
        import jax, jax.numpy as jnp
        import numpy as np
        B, N, D = (4, 2048, 512)
        H, HD = (8, 64)
        key = jax.random.key(seed)
        ks = jax.random.split(key, 6)
        x = jax.random.normal(ks[0], (B, N, D), dtype=jnp.float32)
        adj = (jax.random.uniform(ks[1], (N, N)) < 0.1).astype(jnp.float32)
        adj = jnp.maximum(adj, jnp.eye(N, dtype=jnp.float32))
        s = 0.02
        Wq = jax.random.normal(ks[2], (D, H * HD), dtype=jnp.float32) * s
        Wk = jax.random.normal(ks[3], (D, H * HD), dtype=jnp.float32) * s
        Wv = jax.random.normal(ks[4], (D, H * HD), dtype=jnp.float32) * s
        bq = jnp.zeros((H * HD,), dtype=jnp.float32)
        bk = jnp.zeros((H * HD,), dtype=jnp.float32)
        bv = jnp.zeros((H * HD,), dtype=jnp.float32)
        return {'x': x, 'adj': adj, 'Wq': Wq, 'bq': bq, 'Wk': Wk, 'bk': bk, 'Wv': Wv, 'bv': bv}
    _L0_gnn_all = _L0_gnn_setup()
    _L0_gnn_in = {k: v for k, v in _L0_gnn_all.items() if k in ('Wq', 'bq', 'Wk', 'bk', 'Wv', 'bv', )}
    del _L0_gnn_all

    return {
        "x": x,
        "adj": adj,
        "L0_gnn_Wq": _L0_gnn_in["Wq"],
        "L0_gnn_bq": _L0_gnn_in["bq"],
        "L0_gnn_Wk": _L0_gnn_in["Wk"],
        "L0_gnn_bk": _L0_gnn_in["bk"],
        "L0_gnn_Wv": _L0_gnn_in["Wv"],
        "L0_gnn_bv": _L0_gnn_in["bv"],
    }

def reference(x, adj, L0_gnn_Wq, L0_gnn_bq, L0_gnn_Wk, L0_gnn_bk, L0_gnn_Wv, L0_gnn_bv):
    import jax
    import jax.numpy as jnp
    def _L0_gnn_ref(x, adj, Wq, bq, Wk, bk, Wv, bv):
        import jax, jax.numpy as jnp
        import numpy as np
        B, N, D = (4, 2048, 512)
        H, HD = (8, 64)
        b, n, _ = x.shape
        q = (x @ Wq + bq).reshape(b, n, H, HD)
        k = (x @ Wk + bk).reshape(b, n, H, HD)
        v = (x @ Wv + bv).reshape(b, n, H, HD)
        scores = jnp.einsum('bihd,bjhd->bhij', q, k) / jnp.sqrt(jnp.float32(HD))
        mask = jnp.where(adj == 0, jnp.float32(-1000000000.0), jnp.float32(0.0))
        scores = scores + mask[None, None, :, :]
        weights = jax.nn.softmax(scores, axis=-1)
        out = jnp.einsum('bhij,bjhd->bihd', weights, v)
        return out.reshape(b, n, H * HD)

    h = jnp.maximum(_layernorm(x, axis=-1), 0.0)
    x = x + _L0_gnn_ref(h, adj, L0_gnn_Wq, L0_gnn_bq, L0_gnn_Wk, L0_gnn_bk, L0_gnn_Wv, L0_gnn_bv)
    return x


_drawn_inputs = setup_inputs


def setup_inputs(seed=0):
    import zlib

    import numpy as np

    out = dict(_drawn_inputs(seed))
    spreads = {'L0_gnn_bq': (0.0, 0.8), 'L0_gnn_bk': (0.0, 0.8), 'L0_gnn_bv': (0.0, 0.1)}
    factors = {'L0_gnn_Wq': 7.476, 'L0_gnn_Wk': 6.99}
    for name, (base, spread) in spreads.items():
        noise = np.random.default_rng([zlib.crc32(name.encode()), seed]).standard_normal(out[name].shape)
        drawn = base * np.exp(spread * noise) if base else spread * noise
        out[name] = jnp.asarray(drawn.astype(out[name].dtype))
    for name, factor in factors.items():
        out[name] = (out[name] * factor).astype(out[name].dtype)
    return out
```

```python
from contextlib import ExitStack

import numpy as np

import concourse.bass as bass
from concourse import mybir

F32 = mybir.dt.float32
F32R = mybir.dt.float32r
BF16 = mybir.dt.bfloat16
ALU = mybir.AluOpType
ACT = mybir.ActivationFunctionType
AX = mybir.AxisListType

P = 128
B, N, D, H = 16, 1024, 512, 8
HD = D // H
C = D // P
NB = N // P
PAIRS = H // 2
GROUPS = 2 * H
GB = NB // 2
UNITS = GROUPS * NB
SBLOCKS = H * NB
SCALE = float(HD) ** -0.5
EPS = 1e-5
MASKED = 1.0e9
HALF = N // 2

RING = 8
LEAD = 5
LAG = 2

QK_AT = {32 * p + s: (p, k) for p in range(PAIRS) for k, s in enumerate((5, 9, 13, 17))}
HT_SLOTS = (83, 86, 88, 92, 96, 99, 103, 107)
HT_AT = {s: t for t, s in enumerate(HT_SLOTS)}
STATS_AT = {s - 4: t for t, s in enumerate(HT_SLOTS)}
V_FROM = UNITS - 6
V_AT = {V_FROM + j: (1, j) for j in range(6)} | {0: (0, 6), 1: (0, 7)}
V_SPLIT_AT = {s + 1: v for s, v in V_AT.items() if s + 1 < UNITS} | {0: (0, 5)}
XLN = 3
XLN_USES = [len(range(r, NB, XLN)) for r in range(XLN)]


def some(n):
    return not (isinstance(n, int) and n <= 0)


def adj_preln_kernel(nc, x, adj, Wq, bq, Wk, bk, Wv, bv, out):
    with ExitStack() as ctx:
        def sb(name, shape, dt=F32):
            return ctx.enter_context(nc.sbuf_tensor(name, shape, dt))

        def sem(name):
            return ctx.enter_context(nc.semaphore(name))

        wqk_dram = nc.dram_tensor("wqk_split", [PAIRS, P, 2 * C * 2 * P], F32, kind="Internal").ap()

        probs = sb("probs", [P, RING, N])
        mask = sb("mask", [P, NB, N], BF16)
        hT = sb("hT", [P, 2, C, N], F32R)
        vs = sb("vs", [P, NB, H, 2 * HD], F32R)
        qA = sb("qA", [P, N], F32R)
        k1A = sb("k1A", [P, N], F32R)
        k2A = sb("k2A", [P, N], F32R)
        qB = sb("qB", [P, 2, N], F32R)
        k1B = sb("k1B", [P, 2, N], F32R)
        k2B = sb("k2B", [P, 2, N], F32R)
        wv = sb("wv", [P, 2, C, D], F32R)
        wqk = sb("wqk", [P, 2, C, 2, P], F32R)
        pT = sb("pT", [P, 2, 2, GB * P], F32R)
        oT = sb("oT", [P, GB * P])
        xres = sb("xres", [P, 2, NB, P])
        xln = sb("xln", [P, XLN, D])
        proj = sb("proj", [P, HALF])
        vb = sb("vb", [P, D])
        bv_all = sb("bv_all", [P, D])
        bqk = sb("bqk", [P, 2, PAIRS])
        ident = sb("ident", [P, P])
        y = sb("y", [P, 2, GB, HD])
        negmax = sb("negmax", [P, RING])
        rowsum = sb("rowsum", [P, 2 * RING])
        rinv = sb("rinv", [P, 2, GB])
        bn = sb("bn", [P, XLN, nc.vector.BN_STATS_DIM])
        mv = sb("mv", [P, XLN, 2])
        rstd = sb("rstd", [P, XLN])
        negmean = sb("negmean", [P, XLN])
        minus_half = sb("minus_half", [P, 1])

        stage = probs[:, 0:6, :].rearrange("p a n -> p (a n)").rearrange(
            "p (w c n) -> p w c n", w=3, c=C)
        wqk_stage = vs[:, :, :, :].rearrange("p a h d -> p (a h d)").rearrange(
            "p (r w c l n) -> p r w c l n", r=PAIRS, w=2, c=C, l=2)

        S = ctx.enter_context(nc.psum_tensor("S", [P, 2, N], F32))
        T = ctx.enter_context(nc.psum_tensor("T", [P, 2, GB * P], F32))
        O = ctx.enter_context(nc.psum_tensor("O", [P, GB * P], F32))
        misc = ctx.enter_context(nc.psum_tensor("misc", [P, D], F32))

        w_in, adj_in, b_in = sem("w_in"), sem("adj_in"), sem("b_in")
        wv_split, wqk_split, wqk_stored = sem("wv_split"), sem("wqk_split"), sem("wqk_stored")
        w_hi, w_used = sem("w_hi"), sem("w_used")
        mask_made, mask_zero, consts, ident_zero = sem("mask_made"), sem("mask_zero"), sem("consts"), sem("ident_zero")
        bias_made = sem("bias_made")
        wqk_in = sem("wqk_in")
        xln_in = [sem(f"xln_in{r}") for r in range(XLN)]
        xres_in = [sem(f"xres_in{r}") for r in range(2)]
        stored = [sem(f"stored{r}") for r in range(2)]
        bn_done, mv_done, ln_part, ln_done = sem("bn_done"), sem("mv_done"), sem("ln_part"), sem("ln_done")
        h_turned, h_hi, h_lo = sem("h_turned"), sem("h_hi"), sem("h_lo")
        qk_mm, qk_evac, qk_ready = sem("qk_mm"), sem("qk_evac"), sem("qk_ready")
        qk_high, qk_natural, k_doubled = sem("qk_high"), sem("qk_natural"), sem("k_doubled")
        v_mm, v_biased, v_hi, v_ready = sem("v_mm"), sem("v_biased"), sem("v_hi"), sem("v_ready")
        scored, shifted, exped = sem("scored"), sem("shifted"), sem("exped")
        turned, p_hi, p_lo, contracted = sem("turned"), sem("p_hi"), sem("p_lo"), sem("contracted")
        o_copied, o_turned, y_summed, y_scaled, y_added = (
            sem("o_copied"), sem("o_turned"), sem("y_summed"), sem("y_scaled"), sem("y_added"))

        dve_passed, gp_passed, sp_passed = sem("dve_passed"), sem("gp_passed"), sem("sp_passed")

        block = ctx.enter_context(nc.Block())

        def qk_buffers(pair, second):
            if not second:
                return qA[:, :], k1A[:, :], k2A[:, :]
            r = pair % 2
            return qB[:, r, :], k1B[:, r, :], k2B[:, r, :]

        def before(b, slot, is_y, last):
            uses = []
            for s in range(slot + 1):
                if s % NB == LAG:
                    uses.append((s, True, y_summed, GROUPS * b + s // NB))
                if s in V_AT and not (last and s >= V_FROM):
                    nxt, j = V_AT[s]
                    uses.append((s, False, v_biased, NB * (b + nxt) + j + 1))
                if s in QK_AT and not (last and QK_AT[s][0] == PAIRS - 1):
                    p, k = QK_AT[s]
                    uses.append((s, False, qk_evac, 4 * (PAIRS * b + p + 1) + k + 1))
                if s in HT_AT and not last:
                    uses.append((s, False, h_lo, NB * (b + 1) + HT_AT[s] + 1))
            at = [n for n, use in enumerate(uses) if use[:2] == (slot, is_y)][0]
            if at == 0:
                return v_biased, NB * b + 6
            return uses[at - 1][2:]

        @block.sync
        def _(sp):
            def load_xln(b, t):
                sp.sem_inc(sp_passed)
                sp.dma_start(xln[:, t % XLN, :], x[b, t * P:(t + 1) * P, :]).then_inc(xln_in[t % XLN], 16)

            def load_xres(b, p):
                sp.sem_inc(sp_passed)
                src = x[b].rearrange("(i t) c -> t i c", t=P)[:, :, p * P:(p + 1) * P]
                sp.dma_start(xres[:, p % 2], src).then_inc(xres_in[p % 2], 16)

            def load_wqk(p):
                sp.dma_start(wqk[:].rearrange("p w c l n -> p (w c l n)").bitcast(F32),
                             wqk_dram[p]).then_inc(wqk_in, 16)

            def store(b, p):
                sp.sem_inc(sp_passed)
                dst = out[b].rearrange("(i t) c -> t i c", t=P)[:, :, p * P:(p + 1) * P]
                sp.dma_start(dst, xres[:, p % 2]).then_inc(stored[p % 2], 16)

            for t in range(XLN):
                sp.dma_start(xln[:, t, :], x[0, t * P:(t + 1) * P, :]).then_inc(xln_in[t], 16)
            for w, src in enumerate((Wq, Wk, Wv)):
                sp.dma_start(stage[:, w], src.rearrange("(c p) n -> p c n", p=P)).then_inc(w_in, 16)
            for w, src in enumerate((bq, bk)):
                sp.dma_start(bqk[:, w, :], src.rearrange("(r p) -> p r", p=P),
                             allow_slow_non_contiguous=True).then_inc(b_in, 16)
            sp.dma_start(bv_all[:], bv.partition_broadcast(P)).then_inc(b_in, 16)
            sp.wait_ge(wqk_split, 4)
            sp.dma_start(wqk_dram.rearrange("r p n -> p r n"),
                         wqk_stage.rearrange("p r w c l n -> p r (w c l n)").bitcast(F32)).then_inc(wqk_stored, 16)
            sp.wait_ge(w_used, 1)
            sp.dma_start(probs[:, :, :], adj.rearrange("(i p) n -> p i n", p=P)).then_inc(adj_in, 16)
            sp.wait_ge(wqk_stored, 16)
            load_wqk(0)
            for t in range(XLN, NB):
                sp.wait_ge(h_turned, t - XLN + 1)
                load_xln(0, t)
            for p in range(2):
                load_xres(0, p)
            sp.wait_ge(qk_mm, 4)
            load_wqk(1)

            def body(b, first=False, last=False):
                for p in range(PAIRS):
                    if not (first and p == 0):
                        sp.wait_ge(y_added, 4 * (PAIRS * b + p))
                        if p == 0:
                            store(b - 1, PAIRS - 1)
                        else:
                            store(b, p - 1)
                        if not (last and p == PAIRS - 1):
                            r = (p + 1) % 2
                            sp.wait_ge(stored[r], 16 * (2 * b + (p + 1) // 2))
                            if p == PAIRS - 1:
                                load_xres(b + 1, 0)
                            else:
                                load_xres(b, p + 1)
                    if not (last and p >= PAIRS - 2):
                        sp.wait_ge(qk_mm, 4 * (PAIRS * b + p + 1) + 4)
                        load_wqk((p + 2) % PAIRS)
                    if last:
                        continue
                    if p == 1:
                        sp.wait_ge(h_turned, NB * (b + 1))
                        for t in range(XLN):
                            load_xln(b + 1, t)
                    if p == 2:
                        for t in range(XLN, NB):
                            sp.wait_ge(h_turned, NB * (b + 1) + t - XLN + 1)
                            load_xln(b + 1, t)

            body(0, first=True)
            with sp.Fori(1, B - 1) as b:
                body(b)
            body(B - 1, last=True)
            sp.wait_ge(y_added, GROUPS * B)
            store(B - 1, PAIRS - 1)
            for r in range(2):
                sp.wait_ge(stored[r], 16 * B * PAIRS // 2)

        @block.gpsimd
        def _(gp):
            gp.memset(ident[:], 0.0).then_inc(ident_zero, 1)
            gp.memset(minus_half[:], -0.5).then_inc(ident_zero, 1)
            gp.wait_ge(ident_zero, 2)
            gp.affine_select(out=ident[:], in_=ident[:], compare_op=ALU.not_equal, fill=1.0, base=0,
                             pattern=[[-1, P]], channel_multiplier=1).then_inc(consts, 1)

            def normalise(b, t):
                r, n = t % XLN, NB * b + t
                gp.wait_ge(mv_done, n + 1)
                gp.sem_inc(gp_passed)
                gp.tensor_scalar(rstd[:, r:r + 1], mv[:, r, 1:2], EPS, None, ALU.add).then_inc(ln_part, 1)
                gp.tensor_scalar(negmean[:, r:r + 1], mv[:, r, 0:1], -1.0, None, ALU.mult).then_inc(ln_part, 1)
                gp.wait_ge(ln_part, 3 * n + 2)
                gp.tensor_tensor(rstd[:, r:r + 1], rstd[:, r:r + 1], minus_half[:], ALU.pow).then_inc(ln_part, 1)
                gp.wait_ge(ln_part, 3 * n + 3)
                gp.sem_inc(gp_passed)
                gp.tensor_scalar(xln[:, r, :], xln[:, r, :], negmean[:, r:r + 1], rstd[:, r:r + 1],
                                 ALU.add, ALU.mult).then_inc(ln_done, 1)

            def split_v(b, j):
                gp.wait_ge(v_hi, NB * b + j + 1)
                v3 = vs[:, j, :, :].bitcast(F32)
                gp.tensor_tensor(vs[:, j, :, HD:], vb[:].rearrange("p (h d) -> p h d", h=H),
                                 v3[:, :, :HD], ALU.subtract).then_inc(v_ready, 1)

            def split_qk(b, p, k):
                n = 4 * (PAIRS * b + p) + k
                cols = slice(k // 2 * HALF, (k // 2 + 1) * HALF)
                gp.wait_ge(qk_evac, n + 1)
                gp.sem_inc(gp_passed)
                for second in range(2):
                    q, k1, _ = qk_buffers(p, second)
                    rows = slice(HD * second, HD * second + HD)
                    gp.tensor_copy((k1 if k % 2 else q)[rows, cols], proj[rows, :]).then_inc(qk_high, 1)
                    gp.wait_ge(qk_high, 2 * n + 1 + second)
                    if not (k % 2 and second):
                        gp.sem_inc(gp_passed)
                if k % 2:
                    for second in range(2):
                        _, k1, k2 = qk_buffers(p, second)
                        rows = slice(HD * second, HD * second + HD)
                        gp.tensor_tensor(k2[rows, cols], proj[rows, :], k1[rows, cols].bitcast(F32),
                                         ALU.subtract).then_inc(qk_natural, 1)
                        gp.wait_ge(qk_natural, n + second)
                gp.sem_inc(gp_passed)

            def finish(b, g):
                n, r, p = GROUPS * b + g, g % 2, (g // 4) % 2
                gp.wait_ge(y_summed, n + 1)
                gp.tensor_tensor(y[:, r], y[:, r], rinv[:, r, :].unsqueeze(2).to_broadcast([P, GB, HD]),
                                 ALU.mult).then_inc(y_scaled, 1)
                gp.wait_ge(y_scaled, n + 1)
                if g % 4 == 0:
                    gp.wait_ge(xres_in[p], 16 * (2 * b + (g // 8) + 1))
                cols = HD * ((g // 2) % 2)
                dst = xres[:, p, GB * (g % 2):GB * (g % 2) + GB, cols:cols + HD]
                gp.tensor_tensor(dst, dst, y[:, r], ALU.add).then_inc(y_added, 1)

            for t in range(NB):
                normalise(0, t)
            for k in range(4):
                split_qk(0, 0, k)
            for j in range(5):
                split_v(0, j)

            def body(b, first=False, last=False):
                for u in range(UNITS):
                    if u in STATS_AT and not last:
                        normalise(b + 1, STATS_AT[u])
                    if u in V_SPLIT_AT and not (last and u > V_FROM):
                        nxt, j = V_SPLIT_AT[u]
                        split_v(b + nxt, j)
                    if u in QK_AT and not (last and QK_AT[u][0] == PAIRS - 1):
                        split_qk(b, QK_AT[u][0] + 1, QK_AT[u][1])
                    if u % NB == LAG and not (first and u == LAG):
                        if u == LAG:
                            finish(b - 1, GROUPS - 1)
                        else:
                            finish(b, u // NB - 1)

            body(0, first=True)
            with gp.Fori(1, B - 1) as b:
                body(b)
            body(B - 1, last=True)
            finish(B - 1, GROUPS - 1)

        @block.tensor
        def _(pe):
            def turn_h(b, t, free=None):
                pe.wait_ge(ln_done, NB * b + t + 1)
                if free:
                    pe.wait_ge(*free)
                for c in range(C):
                    mm = pe.transpose(misc[:, c * P:(c + 1) * P], xln[:, t % XLN, c * P:(c + 1) * P], ident[:])
                mm.then_inc(h_turned, 1)

            def project_qk(b, p, k, free):
                w, half = k % 2, k // 2
                pair = PAIRS * b + p
                cols = slice(half * HALF, (half + 1) * HALF)
                pe.wait_ge(h_lo, NB * (b + p // PAIRS) + GB * (half + 1))
                pe.wait_ge(wqk_in, 16 * (pair + 1))
                pe.wait_ge(*free)
                parts = [(c, wl, hl) for c in range(C) for wl, hl in ((0, 0), (0, 1), (1, 0))]
                for n, (c, wl, hl) in enumerate(parts):
                    mm = pe.matmul(misc[:], wqk[:, w, c, wl, :], hT[:, hl, c, cols],
                                   start=n == 0, stop=n == len(parts) - 1)
                mm.then_inc(qk_mm, 1)

            def project_v(b, j, free):
                pe.wait_ge(h_lo, NB * (b + 1))
                pe.wait_ge(*free)
                if isinstance(b, int) and b == 0:
                    pe.wait_ge(wv_split, 1)
                parts = [(c, wl, hl) for c in range(C) for wl, hl in ((0, 0), (1, 0), (0, 1))]
                for n, (c, wl, hl) in enumerate(parts):
                    mm = pe.matmul(misc[:], hT[:, hl, c, j * P:(j + 1) * P], wv[:, wl, c, :],
                                   start=n == 0, stop=n == len(parts) - 1)
                mm.then_inc(v_mm, 1)

            def score(b, s):
                n = SBLOCKS * b + s
                q, k1, k2 = qk_buffers(s // 16, (s // 8) % 2)
                i = s % NB
                pe.wait_ge(qk_ready, 4 * (PAIRS * b + s // 16 + 1))
                if some(n - 1):
                    pe.wait_ge(exped, n - 1)
                for half in range(2):
                    cols = slice(half * HALF, (half + 1) * HALF)
                    dst = S[:, s % 2, cols]
                    pe.matmul(dst, q[:, i * P:(i + 1) * P], k1[:, cols], start=True, stop=False)
                    mm = pe.matmul(dst, q[:, i * P:(i + 1) * P], k2[:, cols], start=False, stop=True)
                mm.then_inc(scored, 1)

            def turn_probs(b, u):
                n, g, j = UNITS * b + u, u // NB, u % NB
                if j == 0:
                    pe.wait_ge(exped, GB * (GROUPS * b + g + 1))
                if some(n - 1):
                    pe.wait_ge(p_lo, n - 1)
                for i in range(GB):
                    mm = pe.transpose(T[:, u % 2, i * P:(i + 1) * P],
                                      probs[:, (GB * g + i) % RING, j * P:(j + 1) * P], ident[:])
                mm.then_inc(turned, 1)

            def contract(b, u):
                n, g, j, head = UNITS * b + u, u // NB, u % NB, u // (2 * NB)
                if g == 0:
                    pe.wait_ge(v_ready, NB * b + j + 1)
                if j == 0 and some(GROUPS * b + g):
                    pe.wait_ge(o_copied, GROUPS * b + g)
                pe.wait_ge(p_lo, n + 1)
                for part in range(2):
                    mm = pe.matmul(O[:], vs[:, j, head, :], pT[:, u % 2, part, :],
                                   start=(j == 0 and part == 0), stop=(j == NB - 1 and part == 1))
                mm.then_inc(contracted, 1)

            def turn_out(b, g, free):
                pe.wait_ge(o_copied, GROUPS * b + g + 1)
                pe.wait_ge(*free)
                for i in range(GB):
                    mm = pe.transpose(misc[:, i * P:(i + 1) * P], oT[:, i * P:(i + 1) * P], ident[:])
                mm.then_inc(o_turned, 1)

            pe.wait_ge(consts, 1)
            for t in range(NB):
                turn_h(0, t, (h_lo, t) if t else None)
            for k in range(4):
                project_qk(0, 0, k, (qk_evac, k) if k else (h_lo, NB))
            for s in range(LEAD):
                score(0, s)
            for j in range(6):
                project_v(0, j, (v_biased, j) if j else (qk_evac, 4))

            def body(b, first=False, last=False):
                for u in range(UNITS):
                    if u < LAG:
                        if not first:
                            contract(b - 1, UNITS - LAG + u)
                    else:
                        contract(b, u - LAG)
                    if u == LAG and not first:
                        turn_out(b - 1, GROUPS - 1, before(b, u, True, last))
                    if u > LAG and u % NB == LAG:
                        turn_out(b, u // NB - 1, before(b, u, True, last))
                    turn_probs(b, u)
                    s = u // 2 + LEAD
                    if u % 2 == 0 and s < SBLOCKS:
                        score(b, s)
                    if u % 2 == 0 and s >= SBLOCKS and not last:
                        score(b + 1, s - SBLOCKS)
                    if u in V_AT and not (last and u >= V_FROM):
                        nxt, j = V_AT[u]
                        project_v(b + nxt, j, before(b, u, False, last))
                    if u in QK_AT and not (last and QK_AT[u][0] == PAIRS - 1):
                        p, k = QK_AT[u]
                        project_qk(b, p + 1, k, before(b, u, False, last))
                    if u in HT_AT and not last:
                        turn_h(b + 1, HT_AT[u], before(b, u, False, last))

            body(0, first=True)
            with pe.Fori(1, B - 1) as b:
                body(b)
            body(B - 1, last=True)
            for u in range(UNITS - LAG, UNITS):
                contract(B - 1, u)
            turn_out(B - 1, GROUPS - 1, (y_summed, GROUPS * B - 1))

        @block.scalar
        def _(act):
            def copy_out(b, g):
                n = GROUPS * b + g
                act.wait_ge(contracted, NB * (n + 1))
                if some(n):
                    act.wait_ge(o_turned, n)
                act.copy(oT[:], O[:]).then_inc(o_copied, 1)

            def probs_hi(b, u):
                n = UNITS * b + u
                act.wait_ge(turned, n + 1)
                if some(n - 1):
                    act.wait_ge(contracted, n - 1)
                act.copy(pT[:, u % 2, 0, :], T[:, u % 2, :]).then_inc(p_hi, 1)

            def exponential(b, s):
                n = SBLOCKS * b + s
                free = NB * (GROUPS * b + s // GB - 1)
                if some(free):
                    act.wait_ge(turned, free)
                act.wait_ge(shifted, n + 1)
                act.activation(probs[:, s % RING, :], S[:, s % 2, :], ACT.Exp, 
                               bias=negmax[:, s % RING:s % RING + 1], scale=-1.0,
                               accum_out=rowsum[:, s % (2 * RING):s % (2 * RING) + 1]).then_inc(exped, 1)

            def evacuate_qk(b, p, k):
                w, pair = k % 2, PAIRS * b + p
                act.wait_ge(qk_mm, 4 * pair + k + 1)
                if some(4 * pair + k):
                    act.wait_ge(qk_ready, 4 * pair + k)
                if k % 2 == 0 and some(4 * pair + k):
                    act.wait_ge(qk_natural, 4 * pair + k)
                act.activation(proj[:], misc[:], ACT.Identity, bias=bqk[:, w, p % PAIRS:p % PAIRS + 1],
                               scale=-SCALE if w == 0 else 1.0).then_inc(qk_evac, 1)

            def double_k(b, p, k, second):
                cols = slice(k // 2 * HALF, (k // 2 + 1) * HALF)
                _, k1, _ = qk_buffers(p, second)
                at = HD if second else 0
                if not second:
                    act.wait_ge(qk_evac, 4 * (PAIRS * b + p) + k + 1)
                act.copy(k1[HD - at:2 * HD - at, cols], proj[at:at + HD, :]).then_inc(k_doubled, 1)

            def h_high(b, t):
                act.wait_ge(h_turned, NB * b + t + 1)
                act.activation(hT[:, 0, :, t * P:(t + 1) * P], misc[:].rearrange("p (c n) -> p c n", c=C),
                               ACT.Relu).then_inc(h_hi, 1)

            def v_high(b, j):
                act.wait_ge(v_biased, NB * b + j + 1)
                act.copy(vs[:, j, :, :HD], vb[:].rearrange("p (h d) -> p h d", h=H)).then_inc(v_hi, 1)

            act.wait_ge(bias_made, 1)
            for t in range(NB):
                h_high(0, t)
            for k in range(4):
                evacuate_qk(0, 0, k)
                if k % 2:
                    double_k(0, 0, k, 0)
                    double_k(0, 0, k, 1)
            for s in range(LEAD - 1):
                exponential(0, s)
            act.wait_ge(wqk_stored, 16)
            for j in range(5):
                v_high(0, j)

            def body(b, first=False, last=False):
                for u in range(UNITS):
                    if u == 1 and not first:
                        copy_out(b - 1, GROUPS - 1)
                    if u > 1 and u % NB == 1:
                        copy_out(b, u // NB - 1)
                    probs_hi(b, u)
                    s = u // 2 + LEAD - 1
                    if u % 2 == 0 and s < SBLOCKS:
                        exponential(b, s)
                    if u % 2 == 0 and s >= SBLOCKS and not last:
                        exponential(b + 1, s - SBLOCKS)
                    if u in V_SPLIT_AT and not (last and u > V_FROM):
                        nxt, j = V_SPLIT_AT[u]
                        v_high(b + nxt, j)
                    if u in QK_AT and not (last and QK_AT[u][0] == PAIRS - 1):
                        evacuate_qk(b, QK_AT[u][0] + 1, QK_AT[u][1])
                    for second in range(2):
                        v = u - 2 - second
                        if v in QK_AT and QK_AT[v][1] % 2 and not (last and QK_AT[v][0] == PAIRS - 1):
                            double_k(b, QK_AT[v][0] + 1, QK_AT[v][1], second)
                    if u in HT_AT and not last:
                        h_high(b + 1, HT_AT[u])

            body(0, first=True)
            with act.Fori(1, B - 1) as b:
                body(b)
            body(B - 1, last=True)
            copy_out(B - 1, GROUPS - 1)

        @block.vector
        def _(dve):
            def stats(b, t):
                r, n = t % XLN, NB * b + t
                dve.wait_ge(xln_in[r], 16 * (XLN_USES[r] * b + t // XLN + 1))
                if some(n - XLN + 1):
                    dve.wait_ge(ln_done, n - XLN + 1)
                dve.bn_stats(bn[:, r, :], xln[:, r, :]).then_inc(bn_done, 1)
                dve.wait_ge(bn_done, n + 1)
                dve.sem_inc(dve_passed)
                dve.bn_aggr(mv[:, r, :], bn[:, r, :]).then_inc(mv_done, 1)

            def h_low(b, t):
                dve.wait_ge(h_hi, NB * b + t + 1)
                cols = slice(t * P, (t + 1) * P)
                dve.scalar_tensor_tensor(hT[:, 1, :, cols], misc[:].rearrange("p (c n) -> p c n", c=C), 0.0,
                                         hT[:, 0, :, cols].bitcast(F32), ALU.max, ALU.subtract).then_inc(h_lo, 1)

            def low_across(b, p, k, second):
                n = 4 * (PAIRS * b + p) + k
                cols = slice(k // 2 * HALF, (k // 2 + 1) * HALF)
                q, k1, k2 = qk_buffers(p, second)
                hi, lo = (k1, k2) if k % 2 else (q, q)
                at = HD if second else 0
                dve.wait_ge(qk_high, 2 * n + 1 + second)
                if second and k % 2:
                    dve.wait_ge(k_doubled, n + 1)
                    dve.wait_ge(qk_natural, n + 1)
                done = dve.tensor_tensor(lo[HD - at:2 * HD - at, cols], proj[at:at + HD, :],
                                         hi[at:at + HD, cols].bitcast(F32), ALU.subtract)
                if second:
                    done.then_inc(qk_ready, 1)

            def bias_v(b, j):
                n = NB * b + j
                dve.wait_ge(v_mm, n + 1)
                if some(n):
                    dve.wait_ge(v_ready, n)
                dve.tensor_tensor(vb[:], misc[:], bv_all[:], ALU.add).then_inc(v_biased, 1)

            def shift(b, s):
                n = SBLOCKS * b + s
                dve.wait_ge(scored, n + 1)
                dve.sem_inc(dve_passed)
                dve.tensor_tensor_reduce(S[:, s % 2, :], S[:, s % 2, :], mask[:, s % NB, :], 1.0,
                                         3.0e38, ALU.add, ALU.min,
                                         negmax[:, s % RING:s % RING + 1]).then_inc(shifted, 1)

            def probs_low(b, u):
                dve.wait_ge(p_hi, UNITS * b + u + 1)
                dve.tensor_tensor(pT[:, u % 2, 1, :], T[:, u % 2, :], pT[:, u % 2, 0, :].bitcast(F32),
                                  ALU.subtract).then_inc(p_lo, 1)

            def sum_parts(b, g):
                n, r = GROUPS * b + g, g % 2
                if some(n - 1):
                    dve.wait_ge(y_added, n - 1)
                dve.wait_ge(exped, GB * (n + 1))
                at = GB * g % (2 * RING)
                dve.reciprocal(rinv[:, r, :], rowsum[:, at:at + GB])
                dve.wait_ge(o_turned, n + 1)
                dve.tensor_reduce(y[:, r], misc[:].rearrange("p (i l d) -> p i d l", i=GB, l=2),
                                  AX.X, ALU.add).then_inc(y_summed, 1)

            dve.wait_ge(b_in, 48)
            dve.tensor_scalar(bqk[:, 0, :], bqk[:, 0, :], -SCALE, None, ALU.mult).then_inc(bias_made, 1)
            dve.wait_ge(w_in, 48)
            for w in range(2):
                src = stage[:, w].rearrange("p c (r n) -> p c r n", r=PAIRS)
                for r in range(PAIRS):
                    hi = dve.tensor_copy(wqk_stage[:, r, w, :, 0, :], src[:, :, r, :])
                hi.then_inc(w_hi, 1)
            dve.tensor_copy(wv[:, 0], stage[:, 2]).then_inc(w_hi, 1)
            dve.wait_ge(w_hi, 3)
            for w in range(2):
                src = stage[:, w].rearrange("p c (r n) -> p c r n", r=PAIRS)
                for r in range(PAIRS):
                    lo = dve.tensor_tensor(wqk_stage[:, r, w, :, 1, :], src[:, :, r, :],
                                           wqk_stage[:, r, w, :, 0, :].bitcast(F32), ALU.subtract)
                lo.then_inc(wqk_split, 2)
            dve.tensor_tensor(wv[:, 1], stage[:, 2], wv[:, 0].bitcast(F32), ALU.subtract).then_inc(wv_split, 1)
            dve.wait_ge(wv_split, 1)
            dve.sem_inc(w_used, 1)
            for t in range(NB):
                stats(0, t)
                if t >= 1:
                    h_low(0, t - 1)
            h_low(0, NB - 1)
            dve.wait_ge(adj_in, 16)
            for i in range(NB):
                last = dve.tensor_scalar(mask[:, i, :], probs[:, i, :], 0.0, MASKED, ALU.is_equal, ALU.mult)
            last.then_inc(mask_made, 1)
            dve.wait_ge(mask_made, 1)
            for k in range(4):
                low_across(0, 0, k, 0)
                low_across(0, 0, k, 1)
            for s in range(LEAD):
                shift(0, s)
            for j in range(6):
                bias_v(0, j)

            def body(b, first=False, last=False):
                for u in range(UNITS):
                    if u == LAG and not first:
                        sum_parts(b - 1, GROUPS - 1)
                    if u > LAG and u % NB == LAG:
                        sum_parts(b, u // NB - 1)
                    probs_low(b, u)
                    s = u // 2 + LEAD
                    if u % 2 == 0 and s < SBLOCKS:
                        shift(b, s)
                    if u % 2 == 0 and s >= SBLOCKS and not last:
                        shift(b + 1, s - SBLOCKS)
                    if u in V_AT and not (last and u >= V_FROM):
                        nxt, j = V_AT[u]
                        bias_v(b + nxt, j)
                    for second in range(2):
                        v = u - 2 - second
                        if v in QK_AT and not (last and QK_AT[v][0] == PAIRS - 1):
                            low_across(b, QK_AT[v][0] + 1, QK_AT[v][1], second)
                    if u - 1 in HT_AT and not last:
                        h_low(b + 1, HT_AT[u - 1])
                    if u in STATS_AT and not last:
                        stats(b + 1, STATS_AT[u])

            body(0, first=True)
            with dve.Fori(1, B - 1) as b:
                body(b)
            body(B - 1, last=True)
            sum_parts(B - 1, GROUPS - 1)


_INS = ["x", "adj", "L0_gnn_Wq", "L0_gnn_bq", "L0_gnn_Wk", "L0_gnn_bk", "L0_gnn_Wv", "L0_gnn_bv"]


def kernel(**inputs):
    import concourse.bacc as bacc
    from concourse.bass_utils import run_bass_kernel_spmd

    nc = bacc.Bacc("TRN2", target_bir_lowering=False, num_devices=1)
    arrays, args = {}, []
    for name in _INS:
        a = np.ascontiguousarray(inputs[name])
        arrays[f"in_{name}"] = a
        args.append(nc.dram_tensor(f"in_{name}", a.shape, mybir.dt.from_np(a.dtype), kind="ExternalInput").ap())
    args.append(nc.dram_tensor("out_0", (B, N, D), F32, kind="ExternalOutput").ap())
    adj_preln_kernel(nc, *args)
    r = run_bass_kernel_spmd(nc, [arrays], core_ids=[0])
    return r.results[0]["out_0"]
```

```python
from contextlib import ExitStack

import numpy as np

import concourse.bass as bass
from concourse import mybir

F32 = mybir.dt.float32
F32R = mybir.dt.float32r
BF16 = mybir.dt.bfloat16
ALU = mybir.AluOpType
ACT = mybir.ActivationFunctionType
AX = mybir.AxisListType

P = 128
B, N, D, H = 16, 1024, 512, 8
HD = D // H
C = D // P
NB = N // P
PAIRS = H // 2
GROUPS = 2 * H
GB = NB // 2
UNITS = GROUPS * NB
SBLOCKS = H * NB
SCALE = float(HD) ** -0.5
EPS = 1e-5
MASKED = 1.0e9
HALF = N // 2

RING = 8
LEAD = 5
LAG = 2
PT = 3

QK_SLOTS = ((4, 6), (8, 9), (12, 14), (16, 17))
QK_START = {32 * p + s: (p, k) for p in range(PAIRS) for k, (s, _) in enumerate(QK_SLOTS)}
QK_AT = {32 * p + s: (p, k) for p in range(PAIRS) for k, (_, s) in enumerate(QK_SLOTS)}
HT_SLOTS = (83, 85, 87, 89, 91, 93, 95, 97)
HT_AT = {s: t for t, s in enumerate(HT_SLOTS)}
NORM_AT = {s - 2: t for t, s in enumerate(HT_SLOTS)}
STATS_SLOTS = ((5, 7, 15), (37, 39, 47), (69, 71))
STATS_AT = {s: t for t, s in enumerate(sum(STATS_SLOTS, ()))}
STATS_TILES = [[STATS_AT[s] for s in slots] for slots in STATS_SLOTS]
V_SLOTS = (121, 123, 124, 125, 126, 127)
V_FROM = V_SLOTS[0]
V_EARLY = len(V_SLOTS)
V_AT = {s: (1, j) for j, s in enumerate(V_SLOTS)} | {j: (0, V_EARLY + j) for j in range(NB - V_EARLY)}
V_SPLIT_AT = {s + 1: v for s, v in V_AT.items() if s + 1 < UNITS} | {0: (0, V_EARLY - 1)}
XLN = 2
XLN_USES = [len(range(r, NB, XLN)) for r in range(XLN)]


def some(n):
    return not (isinstance(n, int) and n <= 0)


def adj_preln_kernel(nc, x, adj, Wq, bq, Wk, bk, Wv, bv, out):
    with ExitStack() as ctx:
        def sb(name, shape, dt=F32):
            return ctx.enter_context(nc.sbuf_tensor(name, shape, dt))

        def sem(name):
            return ctx.enter_context(nc.semaphore(name))

        wqk_dram = nc.dram_tensor("wqk_split", [PAIRS, P, 2 * C * 2 * P], F32, kind="Internal").ap()

        probs = sb("probs", [P, RING, N])
        mask = sb("mask", [P, NB, N], BF16)
        hT = sb("hT", [P, 2, C, N], F32R)
        vs = sb("vs", [P, NB, H, 2 * HD], F32R)
        qA = sb("qA", [P, N], F32R)
        kA = sb("kA", [P, 2, N], F32R)
        qB = sb("qB", [P, 2, N], F32R)
        kB = sb("kB", [P, 2, 2, N], F32R)
        wv = sb("wv", [P, 2, C, D], F32R)
        wqk = sb("wqk", [P, 2, C, 2, P], F32R)
        pT = sb("pT", [P, PT, 2, GB * P], F32R)
        oT = sb("oT", [P, GB * P])
        xres = sb("xres", [P, 2, NB, P])
        xln = sb("xln", [P, XLN, D])
        proj = sb("proj", [P, 2, HALF])
        bv_all = sb("bv_all", [P, D])
        bqk = sb("bqk", [P, 2, PAIRS])
        ident = sb("ident", [P, P])
        yparts = sb("yparts", [P, GB, 2, HD])
        negmax = sb("negmax", [P, RING])
        rowsum = sb("rowsum", [P, 2 * RING])
        rinv = sb("rinv", [P, 2, GB])
        bn = sb("bn", [P, XLN, nc.vector.BN_STATS_DIM])
        mv = sb("mv", [P, NB, 2])
        rstd = sb("rstd", [P, NB])
        negmean = sb("negmean", [P, NB])
        minus_half = sb("minus_half", [P, 1])

        stage = probs[:, 0:6, :].rearrange("p a n -> p (a n)").rearrange(
            "p (w c n) -> p w c n", w=3, c=C)
        wqk_stage = vs[:, 0:6, :, :].rearrange("p a h d -> p (a h d)").rearrange(
            "p (r w c l n) -> p r w c l n", r=PAIRS - 1, w=2, c=C, l=2)
        x0 = [probs[:, 6:8, :].rearrange("p a (t n) -> p (a t) n", n=D),
              xres[:, :, :, :].rearrange("p a i c -> p (a i c)").rearrange("p (t n) -> p t n", n=D)]

        vb = proj[:, 1, :]

        S = ctx.enter_context(nc.psum_tensor("S", [P, 2, N], F32))
        T = ctx.enter_context(nc.psum_tensor("T", [P, 2, GB * P], F32))
        O = ctx.enter_context(nc.psum_tensor("O", [P, GB * P], F32))
        misc = ctx.enter_context(nc.psum_tensor("misc", [P, D], F32))

        w_in, adj_in = [sem(f"w_in{w}") for w in range(3)], [sem(f"adj_in{i}") for i in range(4)]
        x0_in, b_in = [sem(f"x0_in{i}") for i in range(2)], sem("b_in")
        wv_split, wqk_split, wqk_stored = sem("wv_split"), sem("wqk_split"), sem("wqk_stored")
        w0_split = sem("w0_split")
        w_hi = sem("w_hi")
        mask_made, consts, ident_zero = sem("mask_made"), sem("consts"), sem("ident_zero")
        bias_made = sem("bias_made")
        wqk_in = sem("wqk_in")
        xln_in = [sem(f"xln_in{r}") for r in range(XLN)]
        xres_in = [sem(f"xres_in{r}") for r in range(2)]
        stored = [sem(f"stored{r}") for r in range(2)]
        bn_done, mv_done, ln_part, ln_done = sem("bn_done"), sem("mv_done"), sem("ln_part"), sem("ln_done")
        h_turned, h_hi, h_lo = sem("h_turned"), sem("h_hi"), sem("h_lo")
        qk_mm, qk_evac, qk_high = sem("qk_mm"), sem("qk_evac"), sem("qk_high")
        q_low, k_low, k_copied = sem("q_low"), sem("k_low"), sem("k_copied")
        v_mm, v_biased, v_hi, v_ready = sem("v_mm"), sem("v_biased"), sem("v_hi"), sem("v_ready")
        scored, shifted, exped = sem("scored"), sem("shifted"), sem("exped")
        turned, p_hi, p_lo, contracted = sem("turned"), sem("p_hi"), sem("p_lo"), sem("contracted")
        inverted, y_copied = sem("inverted"), sem("y_copied")
        o_copied, o_turned, y_summed, y_scaled, y_added = (
            sem("o_copied"), sem("o_turned"), sem("y_summed"), sem("y_scaled"), sem("y_added"))

        dve_passed, gp_passed, sp_passed = sem("dve_passed"), sem("gp_passed"), sem("sp_passed")

        block = ctx.enter_context(nc.Block())

        def qk_buffers(pair, second):
            if not second:
                return qA[:, :], kA[:, :, :]
            return qB[:, pair % 2, :], kB[:, pair % 2, :, :]

        def x_tile(b, t):
            return xln[:, t % XLN, :] if some(b) else x0[t // GB][:, t % GB, :]

        def before(b, slot, is_y, last):
            uses = []
            for s in range(slot + 1):
                if s in V_AT and not (last and s >= V_FROM):
                    nxt, j = V_AT[s]
                    uses.append((s, False, v_biased, NB * (b + nxt) + j + 1))
                if s in QK_START and not (last and QK_START[s][0] == PAIRS - 1):
                    p, k = QK_START[s]
                    uses.append((s, False, qk_evac, 4 * (PAIRS * b + p + 1) + k + 1))
                if s in HT_AT and not last:
                    uses.append((s, False, h_lo, NB * (b + 1) + HT_AT[s] + 1))
                if s % NB == LAG and some(GROUPS * b + s // NB):
                    uses.append((s, True, y_copied, GROUPS * b + s // NB))
            at = [n for n, use in enumerate(uses) if use[:2] == (slot, is_y)][0]
            if at == 0:
                return v_biased, NB * b + V_EARLY
            return uses[at - 1][2:]

        @block.sync
        def _(sp):
            def load_xln(b, t):
                sp.sem_inc(sp_passed)
                sp.dma_start(xln[:, t % XLN, :], x[b, t * P:(t + 1) * P, :]).then_inc(xln_in[t % XLN], 16)

            def load_xres(b, p):
                sp.sem_inc(sp_passed)
                src = x[b].rearrange("(i t) c -> t i c", t=P)[:, :, p * P:(p + 1) * P]
                sp.dma_start(xres[:, p % 2], src).then_inc(xres_in[p % 2], 16)

            def load_wqk(p):
                sp.dma_start(wqk[:].rearrange("p w c l n -> p (w c l n)").bitcast(F32),
                             wqk_dram[p]).then_inc(wqk_in, 16)

            def copy_k(b, p, half):
                cols = slice(half * HALF, (half + 1) * HALF)
                sp.wait_ge(k_low, 4 * (PAIRS * b + p) + 2 * (half + 1))
                for second in range(2):
                    _, k = qk_buffers(p, second)
                    own, other = (slice(0, HD), slice(HD, P))[::-1 if second else 1]
                    sp.dma_start(k[other, :, cols].bitcast(F32), k[own, :, cols].bitcast(F32)
                                 ).then_inc(k_copied, 16)

            def store(b, p):
                sp.sem_inc(sp_passed)
                dst = out[b].rearrange("(i t) c -> t i c", t=P)[:, :, p * P:(p + 1) * P]
                sp.dma_start(dst, xres[:, p % 2]).then_inc(stored[p % 2], 16)

            for i in range(2):
                src = x[0, i * HALF:(i + 1) * HALF].rearrange("(t p) n -> p t n", p=P)
                sp.dma_start(x0[i], src).then_inc(x0_in[i], 16)
            for w, src in ((1, Wk), (0, Wq), (2, Wv)):
                sp.dma_start(stage[:, w], src.rearrange("(c p) n -> p c n", p=P)).then_inc(w_in[w], 16)
            for w, src in enumerate((bq, bk)):
                sp.dma_start(bqk[:, w, :], src.rearrange("(r p) -> p r", p=P),
                             allow_slow_non_contiguous=True).then_inc(b_in, 16)
            sp.dma_start(bv_all[:], bv.partition_broadcast(P)).then_inc(b_in, 16)
            adj_blocks = adj.rearrange("(i p) n -> p i n", p=P)

            def load_adj(i):
                sp.dma_start(probs[:, 2 * i:2 * i + 2, :], adj_blocks[:, 2 * i:2 * i + 2]).then_inc(adj_in[i], 16)

            sp.wait_ge(h_turned, GB)
            load_adj(3)
            sp.wait_ge(wqk_split, 2)
            load_adj(0)
            load_adj(1)
            sp.dma_start(wqk_dram[0], wqk[:].rearrange("p w c l n -> p (w c l n)").bitcast(F32)
                         ).then_inc(wqk_stored, 16)
            sp.dma_start(wqk_dram[1:].rearrange("r p n -> p r n"),
                         wqk_stage.rearrange("p r w c l n -> p r (w c l n)").bitcast(F32)
                         ).then_inc(wqk_stored, 16)
            sp.wait_ge(wv_split, 1)
            load_adj(2)
            for half in range(2):
                copy_k(0, 0, half)
            sp.wait_ge(h_turned, NB)
            for t in range(XLN):
                load_xln(1, t)
            for p in range(2):
                load_xres(0, p)
            sp.wait_ge(qk_mm, 4)
            sp.wait_ge(wqk_stored, 32)
            load_wqk(1)

            def body(b, first=False, last=False):
                for p in range(PAIRS):
                    if p < len(STATS_SLOTS) and not last:
                        for t in STATS_TILES[p][:2]:
                            if t < XLN and not first:
                                sp.wait_ge(h_turned, NB * (b + 1))
                            if t >= XLN:
                                sp.wait_ge(bn_done, NB * (b + 1) + t - XLN + 1)
                            if not (first and t < XLN):
                                load_xln(b + 1, t)
                    if not (first and p == 0):
                        sp.wait_ge(y_added, 4 * (PAIRS * b + p))
                        if p == 0:
                            store(b - 1, PAIRS - 1)
                        else:
                            store(b, p - 1)
                        if not (last and p == PAIRS - 1):
                            r = (p + 1) % 2
                            sp.wait_ge(stored[r], 16 * (2 * b + (p + 1) // 2))
                            if p == PAIRS - 1:
                                load_xres(b + 1, 0)
                            else:
                                load_xres(b, p + 1)
                    if not (last and p == PAIRS - 1):
                        copy_k(b, p + 1, 0)
                    if p < len(STATS_SLOTS) and not last:
                        for t in STATS_TILES[p][2:]:
                            sp.wait_ge(bn_done, NB * (b + 1) + t - XLN + 1)
                            load_xln(b + 1, t)
                    if p == len(STATS_SLOTS) - 1 and not last:
                        sp.wait_ge(bn_done, NB * (b + 2))
                        for t in range(XLN):
                            load_xln(b + 1, t)
                    if not (last and p == PAIRS - 1):
                        copy_k(b, p + 1, 1)
                    if not (last and p >= PAIRS - 2):
                        sp.wait_ge(qk_mm, 4 * (PAIRS * b + p + 1) + 4)
                        load_wqk((p + 2) % PAIRS)
                    if p == len(STATS_SLOTS) - 1 and not last:
                        for t in range(XLN, NB):
                            sp.wait_ge(h_turned, NB * (b + 1) + t - XLN + 1)
                            load_xln(b + 1, t)

            body(0, first=True)
            with sp.Fori(1, B - 1) as b:
                body(b)
            body(B - 1, last=True)
            sp.wait_ge(y_added, GROUPS * B)
            store(B - 1, PAIRS - 1)
            for r in range(2):
                sp.wait_ge(stored[r], 16 * B * PAIRS // 2)

        @block.gpsimd
        def _(gp):
            gp.memset(ident[:], 0.0).then_inc(ident_zero, 1)
            gp.memset(minus_half[:], -0.5).then_inc(ident_zero, 1)
            gp.wait_ge(ident_zero, 2)
            gp.affine_select(out=ident[:], in_=ident[:], compare_op=ALU.not_equal, fill=1.0, base=0,
                             pattern=[[-1, P]], channel_multiplier=1).then_inc(consts, 1)

            def spread(b, t):
                n = NB * b + t
                gp.wait_ge(mv_done, n + 1)
                gp.sem_inc(gp_passed)
                gp.tensor_scalar(rstd[:, t:t + 1], mv[:, t, 1:2], EPS, None, ALU.add).then_inc(ln_part, 1)
                gp.tensor_scalar(negmean[:, t:t + 1], mv[:, t, 0:1], -1.0, None, ALU.mult).then_inc(ln_part, 1)
                gp.wait_ge(ln_part, 3 * n + 2)
                gp.tensor_tensor(rstd[:, t:t + 1], rstd[:, t:t + 1], minus_half[:], ALU.pow).then_inc(ln_part, 1)

            def normalise(b, t):
                r = t % XLN
                if some(b):
                    gp.wait_ge(xln_in[r], 16 * (XLN_USES[r] * (2 * b - 1) + t // XLN + 1))
                gp.wait_ge(ln_part, 3 * (NB * b + t + 1))
                gp.sem_inc(gp_passed)
                tile = x_tile(b, t)
                gp.tensor_scalar(tile, tile, negmean[:, t:t + 1], rstd[:, t:t + 1],
                                 ALU.add, ALU.mult).then_inc(ln_done, 1)

            def split_v(b, j):
                gp.wait_ge(v_hi, NB * b + j + 1)
                v3 = vs[:, j, :, :].bitcast(F32)
                gp.tensor_tensor(vs[:, j, :, HD:], vb.rearrange("p (h d) -> p h d", h=H),
                                 v3[:, :, :HD], ALU.subtract).then_inc(v_ready, 1)

            def low_k(b, p, k):
                n = 2 * (PAIRS * b + p) + k // 2
                cols = slice(k // 2 * HALF, (k // 2 + 1) * HALF)
                gp.wait_ge(qk_high, 4 * (PAIRS * b + p) * 2 + 2 * k + 2)
                for second in range(2):
                    _, hi_lo = qk_buffers(p, second)
                    rows = slice(HD * second, HD * second + HD)
                    gp.tensor_tensor(hi_lo[rows, 1, cols], proj[rows, k % 2, :],
                                     hi_lo[rows, 0, cols].bitcast(F32), ALU.subtract).then_inc(k_low, 1)
                    gp.wait_ge(k_low, 2 * n + 1 + second)
                gp.sem_inc(gp_passed)

            def finish(b, g):
                n, p = GROUPS * b + g, (g // 4) % 2
                y = yparts[:, :, 0]
                gp.wait_ge(y_copied, n + 1)
                gp.tensor_tensor(y, y, yparts[:, :, 1], ALU.add).then_inc(y_summed, 1)
                gp.wait_ge(inverted, n + 1)
                gp.wait_ge(y_summed, n + 1)
                gp.tensor_tensor(y, y, rinv[:, g % 2, :].unsqueeze(2).to_broadcast([P, GB, HD]),
                                 ALU.mult).then_inc(y_scaled, 1)
                gp.wait_ge(y_scaled, n + 1)
                if g % 4 == 0:
                    gp.wait_ge(xres_in[p], 16 * (2 * b + (g // 8) + 1))
                cols = HD * ((g // 2) % 2)
                dst = xres[:, p, GB * (g % 2):GB * (g % 2) + GB, cols:cols + HD]
                gp.tensor_tensor(dst, dst, y, ALU.add).then_inc(y_added, 1)

            for t in range(NB):
                spread(0, t)
            for t in range(NB):
                normalise(0, t)
            for k in (0, 2):
                low_k(0, 0, k)
            for j in range(V_EARLY - 1):
                split_v(0, j)

            def body(b, first=False, last=False):
                for u in range(UNITS):
                    if u in STATS_AT and not last:
                        spread(b + 1, STATS_AT[u])
                    if u in NORM_AT and not last:
                        normalise(b + 1, NORM_AT[u])
                    if u in V_SPLIT_AT and not (last and u > V_FROM):
                        nxt, j = V_SPLIT_AT[u]
                        split_v(b + nxt, j)
                    if u - 1 in QK_AT and QK_AT[u - 1][1] % 2 == 0 and not (
                            last and QK_AT[u - 1][0] == PAIRS - 1):
                        low_k(b, QK_AT[u - 1][0] + 1, QK_AT[u - 1][1])
                    if u % NB == LAG and not (first and u == LAG):
                        if u == LAG:
                            finish(b - 1, GROUPS - 1)
                        else:
                            finish(b, u // NB - 1)

            body(0, first=True)
            with gp.Fori(1, B - 1) as b:
                body(b)
            body(B - 1, last=True)
            finish(B - 1, GROUPS - 1)

        @block.tensor
        def _(pe):
            def turn_h(b, t, free=None):
                pe.wait_ge(ln_done, NB * b + t + 1)
                if free:
                    pe.wait_ge(*free)
                for c in range(C):
                    mm = pe.transpose(misc[:, c * P:(c + 1) * P], x_tile(b, t)[:, c * P:(c + 1) * P], ident[:])
                mm.then_inc(h_turned, 1)

            def project_qk(b, p, k, part, free=None):
                w, half = 1 - k % 2, k // 2
                pair = PAIRS * b + p
                cols = slice(half * HALF, (half + 1) * HALF)
                if part == 0:
                    pe.wait_ge(h_lo, NB * (b + p // PAIRS) + GB * (half + 1))
                    if some(pair):
                        pe.wait_ge(wqk_in, 16 * pair)
                    else:
                        pe.wait_ge(w0_split, 2)
                    pe.wait_ge(*free)
                parts = [(c, wl, hl) for c in range(C) for wl, hl in ((0, 0), (0, 1), (1, 0))]
                count = len(parts) // 2
                for n in range(part * count, (part + 1) * count):
                    c, wl, hl = parts[n]
                    mm = pe.matmul(misc[:], wqk[:, w, c, wl, :], hT[:, hl, c, cols],
                                   start=n == 0, stop=n == len(parts) - 1)
                if part == 1:
                    mm.then_inc(qk_mm, 1)

            def project_v(b, j, free):
                pe.wait_ge(h_lo, NB * (b + 1))
                pe.wait_ge(*free)
                if isinstance(b, int) and b == 0:
                    pe.wait_ge(wv_split, 1)
                parts = [(c, wl, hl) for c in range(C) for wl, hl in ((0, 0), (1, 0), (0, 1))]
                for n, (c, wl, hl) in enumerate(parts):
                    mm = pe.matmul(misc[:], hT[:, hl, c, j * P:(j + 1) * P], wv[:, wl, c, :],
                                   start=n == 0, stop=n == len(parts) - 1)
                mm.then_inc(v_mm, 1)

            def score(b, s):
                n = SBLOCKS * b + s
                q, k = qk_buffers(s // 16, (s // 8) % 2)
                i = s % NB
                pair = PAIRS * b + s // 16
                pe.wait_ge(q_low, 4 * (pair + 1))
                pe.wait_ge(k_copied, 64 * (pair + 1))
                if some(n - 1):
                    pe.wait_ge(exped, n - 1)
                for half in range(2):
                    cols = slice(half * HALF, (half + 1) * HALF)
                    dst = S[:, s % 2, cols]
                    pe.matmul(dst, q[:, i * P:(i + 1) * P], k[:, 0, cols], start=True, stop=False)
                    mm = pe.matmul(dst, q[:, i * P:(i + 1) * P], k[:, 1, cols], start=False, stop=True)
                mm.then_inc(scored, 1)

            def turn_probs(b, u):
                n, g, j = UNITS * b + u, u // NB, u % NB
                if j == 0:
                    pe.wait_ge(exped, GB * (GROUPS * b + g + 1))
                if some(n - 1):
                    pe.wait_ge(p_lo, n - 1)
                for i in range(GB):
                    mm = pe.transpose(T[:, u % 2, i * P:(i + 1) * P],
                                      probs[:, (GB * g + i) % RING, j * P:(j + 1) * P], ident[:])
                mm.then_inc(turned, 1)

            def contract(b, u):
                n, g, j, head = UNITS * b + u, u // NB, u % NB, u // (2 * NB)
                if g == 0:
                    pe.wait_ge(v_ready, NB * b + j + 1)
                if j == 0 and some(GROUPS * b + g):
                    pe.wait_ge(o_copied, GROUPS * b + g)
                pe.wait_ge(p_lo, n + 1)
                for part in range(2):
                    mm = pe.matmul(O[:], vs[:, j, head, :], pT[:, u % PT, part, :],
                                   start=(j == 0 and part == 0), stop=(j == NB - 1 and part == 1))
                mm.then_inc(contracted, 1)

            def turn_out(b, g, free):
                pe.wait_ge(o_copied, GROUPS * b + g + 1)
                pe.wait_ge(*free)
                for i in range(GB):
                    mm = pe.transpose(misc[:, i * P:(i + 1) * P], oT[:, i * P:(i + 1) * P], ident[:])
                mm.then_inc(o_turned, 1)

            def score_ahead(b, u, last):
                s = u // 2 + LEAD
                if u % 2 == 0 and s < SBLOCKS:
                    score(b, s)
                if u % 2 == 0 and s >= SBLOCKS and not last:
                    score(b + 1, s - SBLOCKS)

            def fill(b, u, last):
                if u in V_AT and not (last and u >= V_FROM):
                    nxt, j = V_AT[u]
                    project_v(b + nxt, j, before(b, u, False, last))
                if u in QK_START and not (last and QK_START[u][0] == PAIRS - 1):
                    p, k = QK_START[u]
                    project_qk(b, p + 1, k, 0, before(b, u, False, last))
                if u in QK_AT and not (last and QK_AT[u][0] == PAIRS - 1):
                    p, k = QK_AT[u]
                    project_qk(b, p + 1, k, 1)
                if u in HT_AT and not last:
                    turn_h(b + 1, HT_AT[u], before(b, u, False, last))

            pe.wait_ge(consts, 1)
            for t in range(NB):
                turn_h(0, t, (h_lo, t) if t else None)
            for k in range(4):
                project_qk(0, 0, k, 0, (qk_evac, k) if k else (h_lo, NB))
                project_qk(0, 0, k, 1)
            for j in range(V_EARLY):
                project_v(0, j, (v_biased, j) if j else (qk_evac, 4))
            for s in range(LEAD):
                score(0, s)

            def body(b, first=False, last=False):
                for u in range(UNITS):
                    if u % NB == LAG:
                        turn_probs(b, u)
                        score_ahead(b, u, last)
                        contract(b, u - LAG)
                        if u == LAG and not first:
                            turn_out(b - 1, GROUPS - 1, before(b, u, True, last))
                        if u > LAG:
                            turn_out(b, u // NB - 1, before(b, u, True, last))
                        continue
                    if u >= LAG:
                        contract(b, u - LAG)
                    elif not first:
                        contract(b - 1, UNITS - LAG + u)
                    turn_probs(b, u)
                    score_ahead(b, u, last)
                    fill(b, u, last)

            body(0, first=True)
            with pe.Fori(1, B - 1) as b:
                body(b)
            body(B - 1, last=True)
            for u in range(UNITS - LAG, UNITS):
                contract(B - 1, u)
            turn_out(B - 1, GROUPS - 1, (y_copied, GROUPS * B - 1))

        @block.scalar
        def _(act):
            def copy_out(b, g):
                n = GROUPS * b + g
                act.wait_ge(contracted, NB * (n + 1))
                if some(n):
                    act.wait_ge(o_turned, n)
                act.copy(oT[:], O[:]).then_inc(o_copied, 1)

            def copy_y(b, g):
                n = GROUPS * b + g
                act.wait_ge(o_turned, n + 1)
                if some(n):
                    act.wait_ge(y_added, n)
                act.copy(yparts[:].rearrange("p i l d -> p (i l d)"), misc[:]).then_inc(y_copied, 1)

            def probs_hi(b, u):
                n = UNITS * b + u
                act.wait_ge(turned, n + 1)
                used = n + 1 - (PT if u >= PT - 1 else PT - 1)
                if some(used):
                    act.wait_ge(contracted, used)
                act.copy(pT[:, u % PT, 0, :], T[:, u % 2, :]).then_inc(p_hi, 1)

            def exponential(b, s):
                n = SBLOCKS * b + s
                free = NB * (GROUPS * b + s // GB - 1)
                if some(free):
                    act.wait_ge(turned, free)
                act.wait_ge(shifted, n + 1)
                act.activation(probs[:, s % RING, :], S[:, s % 2, :], ACT.Exp,
                               bias=negmax[:, s % RING:s % RING + 1], scale=-1.0,
                               accum_out=rowsum[:, s % (2 * RING):s % (2 * RING) + 1]).then_inc(exped, 1)

            def evacuate_qk(b, p, k):
                w, pair = 1 - k % 2, PAIRS * b + p
                act.wait_ge(qk_mm, 4 * pair + k + 1)
                if p == 1 and k == 1:
                    act.wait_ge(v_ready, NB * (b + 1))
                if some(2 * pair + k // 2):
                    act.wait_ge(q_low if k % 2 else k_low, 2 * (2 * pair + k // 2))
                act.activation(proj[:, k % 2], misc[:], ACT.Identity, bias=bqk[:, w, p % PAIRS:p % PAIRS + 1],
                               scale=-SCALE if w == 0 else 1.0).then_inc(qk_evac, 1)

            def high(b, p, k, second):
                cols = slice(k // 2 * HALF, (k // 2 + 1) * HALF)
                q, hi_lo = qk_buffers(p, second)
                rows = slice(HD * second, HD * second + HD)
                if not second:
                    act.wait_ge(qk_evac, 4 * (PAIRS * b + p) + k + 1)
                act.copy(q[rows, cols] if k % 2 else hi_lo[rows, 0, cols],
                         proj[rows, k % 2, :]).then_inc(qk_high, 1)

            def h_high(b, t):
                act.wait_ge(h_turned, NB * b + t + 1)
                act.activation(hT[:, 0, :, t * P:(t + 1) * P], misc[:].rearrange("p (c n) -> p c n", c=C),
                               ACT.Relu).then_inc(h_hi, 1)

            def v_high(b, j):
                act.wait_ge(v_biased, NB * b + j + 1)
                used = UNITS * (b - 1) + UNITS - NB + j + 1
                if some(used):
                    act.wait_ge(contracted, used)
                act.copy(vs[:, j, :, :HD], vb.rearrange("p (h d) -> p h d", h=H)).then_inc(v_hi, 1)

            act.wait_ge(bias_made, 1)
            for t in range(NB):
                h_high(0, t)
            for k in range(4):
                evacuate_qk(0, 0, k)
                high(0, 0, k, 0)
                high(0, 0, k, 1)
            act.wait_ge(wqk_stored, 32)
            for j in range(V_EARLY - 1):
                v_high(0, j)
            for s in range(LEAD - 1):
                exponential(0, s)

            def body(b, first=False, last=False):
                for u in range(UNITS):
                    if u == 1 and not first:
                        copy_out(b - 1, GROUPS - 1)
                    if u > 1 and u % NB == 1:
                        copy_out(b, u // NB - 1)
                    probs_hi(b, u)
                    s = u // 2 + LEAD - 1
                    if u % 2 == 0 and s < SBLOCKS:
                        exponential(b, s)
                    if u % 2 == 0 and s >= SBLOCKS and not last:
                        exponential(b + 1, s - SBLOCKS)
                    if u == LAG and not first:
                        copy_y(b - 1, GROUPS - 1)
                    if u > LAG and u % NB == LAG:
                        copy_y(b, u // NB - 1)
                    if u in V_SPLIT_AT and not (last and u > V_FROM):
                        nxt, j = V_SPLIT_AT[u]
                        v_high(b + nxt, j)
                    if u in QK_AT and not (last and QK_AT[u][0] == PAIRS - 1):
                        evacuate_qk(b, QK_AT[u][0] + 1, QK_AT[u][1])
                    for second in range(2):
                        v = u - second
                        if v in QK_AT and not (last and QK_AT[v][0] == PAIRS - 1):
                            high(b, QK_AT[v][0] + 1, QK_AT[v][1], second)
                    if u in HT_AT and not last:
                        h_high(b + 1, HT_AT[u])

            body(0, first=True)
            with act.Fori(1, B - 1) as b:
                body(b)
            body(B - 1, last=True)
            copy_out(B - 1, GROUPS - 1)
            copy_y(B - 1, GROUPS - 1)

        @block.vector
        def _(dve):
            def stats(b, t):
                r, n = t % XLN, NB * b + t
                if some(b):
                    dve.wait_ge(xln_in[r], 16 * (XLN_USES[r] * 2 * (b - 1) + t // XLN + 1))
                else:
                    dve.wait_ge(x0_in[t // GB], 16)
                dve.bn_stats(bn[:, r, :], x_tile(b, t)).then_inc(bn_done, 1)
                dve.wait_ge(bn_done, n + 1)
                dve.sem_inc(dve_passed)
                dve.bn_aggr(mv[:, t, :], bn[:, r, :]).then_inc(mv_done, 1)

            def h_low(b, t):
                dve.wait_ge(h_hi, NB * b + t + 1)
                cols = slice(t * P, (t + 1) * P)
                dve.scalar_tensor_tensor(hT[:, 1, :, cols], misc[:].rearrange("p (c n) -> p c n", c=C), 0.0,
                                         hT[:, 0, :, cols].bitcast(F32), ALU.max, ALU.subtract).then_inc(h_lo, 1)

            def low_q(b, p, k, second):
                n = 4 * (PAIRS * b + p) + k
                cols = slice(k // 2 * HALF, (k // 2 + 1) * HALF)
                q, _ = qk_buffers(p, second)
                at = HD * second
                dve.wait_ge(qk_high, 2 * n + 1 + second)
                dve.tensor_tensor(q[HD - at:2 * HD - at, cols], proj[at:at + HD, k % 2, :],
                                  q[at:at + HD, cols].bitcast(F32), ALU.subtract).then_inc(q_low, 1)

            def bias_v(b, j):
                n = NB * b + j
                dve.wait_ge(v_mm, n + 1)
                if j == 0:
                    dve.wait_ge(q_low, 4 * (PAIRS * b + 1))
                if some(n):
                    dve.wait_ge(v_ready, n)
                dve.tensor_tensor(vb, misc[:], bv_all[:], ALU.add).then_inc(v_biased, 1)

            def shift(b, s):
                n = SBLOCKS * b + s
                dve.wait_ge(scored, n + 1)
                dve.sem_inc(dve_passed)
                dve.tensor_tensor_reduce(S[:, s % 2, :], S[:, s % 2, :], mask[:, s % NB, :], 1.0,
                                         3.0e38, ALU.add, ALU.min,
                                         negmax[:, s % RING:s % RING + 1]).then_inc(shifted, 1)

            def probs_low(b, u):
                dve.wait_ge(p_hi, UNITS * b + u + 1)
                dve.tensor_tensor(pT[:, u % PT, 1, :], T[:, u % 2, :], pT[:, u % PT, 0, :].bitcast(F32),
                                  ALU.subtract).then_inc(p_lo, 1)

            def invert(b, g):
                n, r = GROUPS * b + g, g % 2
                if some(n - 1):
                    dve.wait_ge(y_added, n - 1)
                dve.wait_ge(exped, GB * (n + 1))
                at = GB * g % (2 * RING)
                dve.reciprocal(rinv[:, r, :], rowsum[:, at:at + GB]).then_inc(inverted, 1)

            dve.wait_ge(b_in, 48)
            dve.tensor_scalar(bqk[:, 0, :], bqk[:, 0, :], -SCALE, None, ALU.mult).then_inc(bias_made, 1)
            for t in range(NB):
                stats(0, t)

            def split_w(w, r):
                src = stage[:, w, :, r * P:(r + 1) * P]
                parts = wqk[:, w] if r == 0 else wqk_stage[:, r - 1, w]
                dve.tensor_copy(parts[:, :, 0, :], src).then_inc(w_hi, 1)
                return src, parts

            for rs in ((0,), range(1, PAIRS)):
                for w in (1, 0):
                    if 0 in rs:
                        dve.wait_ge(w_in[w], 16)
                    for r in rs:
                        src, parts = split_w(w, r)
                        dve.wait_ge(w_hi, 1 + (1 - w) + r * 2 if r == 0 else 2 + (1 - w) * (PAIRS - 1) + r)
                        lo = dve.tensor_tensor(parts[:, :, 1, :], src, parts[:, :, 0, :].bitcast(F32),
                                               ALU.subtract)
                    lo.then_inc(w0_split if 0 in rs else wqk_split, 1)
                if 0 in rs:
                    for t in range(NB):
                        h_low(0, t)
            dve.wait_ge(w_in[2], 16)
            dve.tensor_copy(wv[:, 0], stage[:, 2]).then_inc(w_hi, 1)
            dve.wait_ge(w_hi, 2 * PAIRS + 1)
            dve.tensor_tensor(wv[:, 1], stage[:, 2], wv[:, 0].bitcast(F32), ALU.subtract).then_inc(wv_split, 1)
            for k in (1, 3):
                low_q(0, 0, k, 0)
                low_q(0, 0, k, 1)
            for j in range(V_EARLY):
                bias_v(0, j)
            for i in (3, 0, 1, 2):
                dve.wait_ge(adj_in[i], 16)
                dve.tensor_scalar(mask[:, 2 * i:2 * i + 2, :], probs[:, 2 * i:2 * i + 2, :], 0.0, MASKED,
                                  ALU.is_equal, ALU.mult).then_inc(mask_made, 1)
            dve.wait_ge(mask_made, 4)
            for s in range(LEAD):
                shift(0, s)

            def body(b, first=False, last=False):
                for u in range(UNITS):
                    if u == LAG and not first:
                        invert(b - 1, GROUPS - 1)
                    if u > LAG and u % NB == LAG:
                        invert(b, u // NB - 1)
                    if u - 1 in HT_AT and not last:
                        h_low(b + 1, HT_AT[u - 1])
                    probs_low(b, u)
                    s = u // 2 + LEAD
                    if u % 2 == 0 and s < SBLOCKS:
                        shift(b, s)
                    if u % 2 == 0 and s >= SBLOCKS and not last:
                        shift(b + 1, s - SBLOCKS)
                    if u in V_AT and not (last and u >= V_FROM):
                        bias_v(b + V_AT[u][0], V_AT[u][1])
                    for second in range(2):
                        v = u - 1 - second
                        if v in QK_AT and QK_AT[v][1] % 2 and not (last and QK_AT[v][0] == PAIRS - 1):
                            low_q(b, QK_AT[v][0] + 1, QK_AT[v][1], second)
                    if u in STATS_AT and not last:
                        stats(b + 1, STATS_AT[u])

            body(0, first=True)
            with dve.Fori(1, B - 1) as b:
                body(b)
            body(B - 1, last=True)
            invert(B - 1, GROUPS - 1)


_INS = ["x", "adj", "L0_gnn_Wq", "L0_gnn_bq", "L0_gnn_Wk", "L0_gnn_bk", "L0_gnn_Wv", "L0_gnn_bv"]


def kernel(**inputs):
    import concourse.bacc as bacc
    from concourse.bass_utils import run_bass_kernel_spmd

    nc = bacc.Bacc("TRN2", target_bir_lowering=False, num_devices=1)
    arrays, args = {}, []
    for name in _INS:
        a = np.ascontiguousarray(inputs[name])
        arrays[f"in_{name}"] = a
        args.append(nc.dram_tensor(f"in_{name}", a.shape, mybir.dt.from_np(a.dtype), kind="ExternalInput").ap())
    args.append(nc.dram_tensor("out_0", (B, N, D), F32, kind="ExternalOutput").ap())
    adj_preln_kernel(nc, *args)
    r = run_bass_kernel_spmd(nc, [arrays], core_ids=[0])
    return r.results[0]["out_0"]
```

```python
from contextlib import ExitStack

import numpy as np

import concourse.bass as bass
from concourse import mybir

F32 = mybir.dt.float32
F32R = mybir.dt.float32r
BF16 = mybir.dt.bfloat16
ALU = mybir.AluOpType
ACT = mybir.ActivationFunctionType

P = 128
B, N, D, H = 16, 1024, 512, 8
HD = D // H
C = D // P
NB = N // P
PAIRS = H // 2
GROUPS = 2 * H
GB = NB // 2
UNITS = GROUPS * NB
SBLOCKS = H * NB
SCALE = float(HD) ** -0.5
EPS = 1e-5
MASKED = 1.0e9
HALF = N // 2

RING = 8
LEAD = 5
LAG = 2
PT = 3

QK_SLOTS = ((4, 6), (8, 9), (12, 14), (16, 17))
QK_START = {32 * p + s: (p, k) for p in range(PAIRS) for k, (s, _) in enumerate(QK_SLOTS)}
QK_AT = {32 * p + s: (p, k) for p in range(PAIRS) for k, (_, s) in enumerate(QK_SLOTS)}
HIGH_AFTER = (1, 2)
LOW_AFTER = (2, 4)
HT_SLOTS = (83, 85, 87, 88, 91, 92, 95, 96)
HT_AT = {s: t for t, s in enumerate(HT_SLOTS)}
NORM_AT = {s - 2: t for t, s in enumerate(HT_SLOTS)}
STATS_SLOTS = ((5, 7, 15), (37, 39, 47), (69, 71))
STATS_AT = {s: t for t, s in enumerate(sum(STATS_SLOTS, ()))}
STATS_TILES = [[STATS_AT[s] for s in slots] for slots in STATS_SLOTS]
V_SLOTS = (121, 123, 124, 125, 126, 127)
V_FROM = V_SLOTS[0]
V_EARLY = len(V_SLOTS)
V_AT = {s: (1, j) for j, s in enumerate(V_SLOTS)} | {j: (0, V_EARLY + j) for j in range(NB - V_EARLY)}
V_SPLIT_AT = {s + 1: v for s, v in V_AT.items() if s + 1 < UNITS} | {0: (0, V_EARLY - 1)}
XLN = 2
XLN_USES = [len(range(r, NB, XLN)) for r in range(XLN)]


def some(n):
    return not (isinstance(n, int) and n <= 0)


def adj_preln_kernel(nc, x, adj, Wq, bq, Wk, bk, Wv, bv, out):
    with ExitStack() as ctx:
        def sb(name, shape, dt=F32):
            return ctx.enter_context(nc.sbuf_tensor(name, shape, dt))

        def sem(name):
            return ctx.enter_context(nc.semaphore(name))

        wqk_dram = nc.dram_tensor("wqk_split", [PAIRS, P, 2 * C * 2 * P], F32, kind="Internal").ap()

        probs = sb("probs", [P, RING, N])
        mask = sb("mask", [P, NB, N], BF16)
        hT = sb("hT", [P, 2, C, N], F32R)
        vs = sb("vs", [P, NB, H, 2 * HD], F32R)
        qA = sb("qA", [P, N], F32R)
        kA = sb("kA", [P, 2, N], F32R)
        qB = sb("qB", [P, 2, N], F32R)
        kB = sb("kB", [P, 2, 2, N], F32R)
        wv = sb("wv", [P, 2, C, D], F32R)
        wqk = sb("wqk", [P, 2, C, 2, P], F32R)
        pT = sb("pT", [P, PT, 2, GB * P], F32R)
        oT = sb("oT", [P, GB * P])
        xres = sb("xres", [P, 2, NB, P])
        xln = sb("xln", [P, XLN, D])
        proj = sb("proj", [P, 2, HALF])
        bv_all = sb("bv_all", [P, D])
        bqk = sb("bqk", [P, 2, PAIRS])
        ident = sb("ident", [P, P])
        yparts = sb("yparts", [P, GB, 2, HD])
        negmax = sb("negmax", [P, RING])
        rowsum = sb("rowsum", [P, 2 * RING])
        rinv = sb("rinv", [P, 2, GB])
        bn = sb("bn", [P, XLN, nc.vector.BN_STATS_DIM])
        mv = sb("mv", [P, NB, 2])
        rstd = sb("rstd", [P, NB])
        negmean = sb("negmean", [P, NB])
        minus_half = sb("minus_half", [P, 1])

        stage = probs[:, 0:6, :].rearrange("p a n -> p (a n)").rearrange(
            "p (w c n) -> p w c n", w=3, c=C)
        wqk_stage = vs[:, 2:8, :, :].rearrange("p a h d -> p (a h d)").rearrange(
            "p (r w c l n) -> p r w c l n", r=PAIRS - 1, w=2, c=C, l=2)
        x0 = [probs[:, 6:8, :].rearrange("p a (t n) -> p (a t) n", n=D),
              xres[:, :, :, :].rearrange("p a i c -> p (a i c)").rearrange("p (t n) -> p t n", n=D)]

        S = ctx.enter_context(nc.psum_tensor("S", [P, 2, N], F32))
        T = ctx.enter_context(nc.psum_tensor("T", [P, 2, GB * P], F32))
        O = ctx.enter_context(nc.psum_tensor("O", [P, GB * P], F32))
        misc = ctx.enter_context(nc.psum_tensor("misc", [P, D], F32))

        h_banks = [S[:, i, half * HALF:(half + 1) * HALF] for i in range(2) for half in range(2)]
        mm_banks = [T[:, 0, :], T[:, 1, :], O[:], misc[:]]

        w_in, adj_in = [sem(f"w_in{w}") for w in range(3)], [sem(f"adj_in{i}") for i in range(4)]
        x0_in, b_in = [sem(f"x0_in{i}") for i in range(4)], sem("b_in")
        wv_split, wqk_split = sem("wv_split"), sem("wqk_split")
        wqk_stored = [sem(f"wqk_stored{r}") for r in range(PAIRS)]
        w0_split = sem("w0_split")
        w_hi, wv_hi = sem("w_hi"), sem("wv_hi")
        mask_made, consts, ident_zero = sem("mask_made"), sem("consts"), sem("ident_zero")
        bias_made = sem("bias_made")
        wqk_in = sem("wqk_in")
        xln_in = [sem(f"xln_in{r}") for r in range(XLN)]
        xres_in = [sem(f"xres_in{r}") for r in range(2)]
        stored = [sem(f"stored{r}") for r in range(2)]
        bn_done, mv_done, ln_part, ln_done = sem("bn_done"), sem("mv_done"), sem("ln_part"), sem("ln_done")
        h_turned, h_hi, h_lo = sem("h_turned"), sem("h_hi"), sem("h_lo")
        qk_mm, qk_evac, qk_high = sem("qk_mm"), sem("qk_evac"), sem("qk_high")
        q_low, k_low, k_copied = sem("q_low"), sem("k_low"), sem("k_copied")
        v_mm, v_biased, v_hi, v_ready = sem("v_mm"), sem("v_biased"), sem("v_hi"), sem("v_ready")
        scored, shifted, exped = sem("scored"), sem("shifted"), sem("exped")
        turned, p_hi, p_lo, contracted = sem("turned"), sem("p_hi"), sem("p_lo"), sem("contracted")
        inverted, y_copied = sem("inverted"), sem("y_copied")
        o_copied, o_turned, y_summed, y_scaled, y_added = (
            sem("o_copied"), sem("o_turned"), sem("y_summed"), sem("y_scaled"), sem("y_added"))

        dve_passed, gp_passed, sp_passed = sem("dve_passed"), sem("gp_passed"), sem("sp_passed")

        block = ctx.enter_context(nc.Block())

        def qk_buffers(pair, second):
            if not second:
                return qA[:, :], kA[:, :, :]
            return qB[:, pair % 2, :], kB[:, pair % 2, :, :]

        def x_tile(b, t):
            return xln[:, t % XLN, :] if some(b) else x0[t // GB][:, t % GB, :]

        def before(b, slot, is_y, last):
            uses = []
            for s in range(slot + 1):
                if s in V_AT and not (last and s >= V_FROM):
                    nxt, j = V_AT[s]
                    uses.append((s, False, v_biased, NB * (b + nxt) + j + 1))
                if s in QK_START and not (last and QK_START[s][0] == PAIRS - 1):
                    p, k = QK_START[s]
                    uses.append((s, False, qk_evac, 4 * (PAIRS * b + p + 1) + k + 1))
                if s in HT_AT and not last:
                    uses.append((s, False, h_lo, NB * (b + 1) + HT_AT[s] + 1))
                if s % NB == LAG and some(GROUPS * b + s // NB):
                    uses.append((s, True, y_copied, GROUPS * b + s // NB))
            at = [n for n, use in enumerate(uses) if use[:2] == (slot, is_y)][0]
            if at == 0:
                return v_biased, NB * b + V_EARLY
            return uses[at - 1][2:]

        @block.sync
        def _(sp):
            def load_xln(b, t):
                sp.sem_inc(sp_passed)
                sp.dma_start(xln[:, t % XLN, :], x[b, t * P:(t + 1) * P, :]).then_inc(xln_in[t % XLN], 16)

            def load_xres(b, p):
                sp.sem_inc(sp_passed)
                src = x[b].rearrange("(i t) c -> t i c", t=P)[:, :, p * P:(p + 1) * P]
                sp.dma_start(xres[:, p % 2], src).then_inc(xres_in[p % 2], 16)

            def load_wqk(p):
                sp.dma_start(wqk[:].rearrange("p w c l n -> p (w c l n)").bitcast(F32),
                             wqk_dram[p]).then_inc(wqk_in, 16)

            def copy_k(b, p, half):
                cols = slice(half * HALF, (half + 1) * HALF)
                sp.wait_ge(k_low, 4 * (PAIRS * b + p) + 2 * (half + 1))
                for second in range(2):
                    _, k = qk_buffers(p, second)
                    own, other = (slice(0, HD), slice(HD, P))[::-1 if second else 1]
                    sp.dma_start(k[other, :, cols].bitcast(F32), k[own, :, cols].bitcast(F32)
                                 ).then_inc(k_copied, 16)

            def store(b, p):
                sp.sem_inc(sp_passed)
                dst = out[b].rearrange("(i t) c -> t i c", t=P)[:, :, p * P:(p + 1) * P]
                sp.dma_start(dst, xres[:, p % 2]).then_inc(stored[p % 2], 16)

            for w, src in enumerate((bq, bk)):
                sp.dma_start(bqk[:, w, :], src.rearrange("(r p) -> p r", p=P),
                             allow_slow_non_contiguous=True).then_inc(b_in, 16)
            sp.dma_start(bv_all[:], bv.partition_broadcast(P)).then_inc(b_in, 16)
            for i in range(4):
                src = x[0, 2 * i * P:(2 * i + 2) * P].rearrange("(t p) n -> p t n", p=P)
                sp.dma_start(x0[i // 2][:, 2 * (i % 2):2 * (i % 2) + 2], src).then_inc(x0_in[i], 16)
            for w, src in ((1, Wk), (0, Wq), (2, Wv)):
                sp.dma_start(stage[:, w], src.rearrange("(c p) n -> p c n", p=P)).then_inc(w_in[w], 16)
            adj_blocks = adj.rearrange("(i p) n -> p i n", p=P)

            def load_adj(i):
                blocks = slice(2 * i, 2 * i + 2)
                sp.dma_start(probs[:, blocks, :], adj_blocks[:, blocks]).then_inc(adj_in[i], 16)

            sp.wait_ge(h_turned, GB)
            load_adj(3)
            for w in (1, 0):
                sp.wait_ge(w0_split, 2 - w)
                sp.wait_ge(wqk_split, (PAIRS - 1) * (2 - w))
                load_adj(w)
            sp.wait_ge(wv_split, 1)
            load_adj(2)

            def store_wqk(r):
                src = (wqk[:] if r == 0 else wqk_stage[:, r - 1]).rearrange("p w c l n -> p (w c l n)")
                sp.dma_start(wqk_dram[r], src.bitcast(F32)).then_inc(wqk_stored[r], 16)

            store_wqk(1)
            store_wqk(2)
            for half in range(2):
                copy_k(0, 0, half)
            store_wqk(3)
            store_wqk(0)
            sp.wait_ge(h_turned, NB)
            for t in range(XLN):
                load_xln(1, t)
            for p in range(2):
                load_xres(0, p)
            sp.wait_ge(qk_mm, 4)
            for r in range(PAIRS):
                sp.wait_ge(wqk_stored[r], 16)
            load_wqk(1)

            def body(b, first=False, last=False):
                for p in range(PAIRS):
                    if p < len(STATS_SLOTS) and not last:
                        for t in STATS_TILES[p][:2]:
                            if t < XLN and not first:
                                sp.wait_ge(h_turned, NB * (b + 1))
                            if t >= XLN:
                                sp.wait_ge(bn_done, NB * (b + 1) + t - XLN + 1)
                            if not (first and t < XLN):
                                load_xln(b + 1, t)
                    if not (first and p == 0):
                        sp.wait_ge(y_added, 4 * (PAIRS * b + p))
                        if p == 0:
                            store(b - 1, PAIRS - 1)
                        else:
                            store(b, p - 1)
                        if not (last and p == PAIRS - 1):
                            r = (p + 1) % 2
                            sp.wait_ge(stored[r], 16 * (2 * b + (p + 1) // 2))
                            if p == PAIRS - 1:
                                load_xres(b + 1, 0)
                            else:
                                load_xres(b, p + 1)
                    if not (last and p == PAIRS - 1):
                        copy_k(b, p + 1, 0)
                    if p < len(STATS_SLOTS) and not last:
                        for t in STATS_TILES[p][2:]:
                            sp.wait_ge(bn_done, NB * (b + 1) + t - XLN + 1)
                            load_xln(b + 1, t)
                    if p == len(STATS_SLOTS) - 1 and not last:
                        sp.wait_ge(bn_done, NB * (b + 2))
                        for t in range(XLN):
                            load_xln(b + 1, t)
                    if not (last and p == PAIRS - 1):
                        copy_k(b, p + 1, 1)
                    if not (last and p >= PAIRS - 2):
                        sp.wait_ge(qk_mm, 4 * (PAIRS * b + p + 1) + 4)
                        load_wqk((p + 2) % PAIRS)
                    if p == len(STATS_SLOTS) - 1 and not last:
                        for t in range(XLN, NB):
                            sp.wait_ge(h_turned, NB * (b + 1) + t - XLN + 1)
                            load_xln(b + 1, t)

            body(0, first=True)
            with sp.Fori(1, B - 1) as b:
                body(b)
            body(B - 1, last=True)
            sp.wait_ge(y_added, GROUPS * B)
            store(B - 1, PAIRS - 1)
            for r in range(2):
                sp.wait_ge(stored[r], 16 * B * PAIRS // 2)

        @block.gpsimd
        def _(gp):
            gp.memset(ident[:], 0.0).then_inc(ident_zero, 1)
            gp.memset(minus_half[:], -0.5).then_inc(ident_zero, 1)
            gp.wait_ge(ident_zero, 2)
            gp.affine_select(out=ident[:], in_=ident[:], compare_op=ALU.not_equal, fill=1.0, base=0,
                             pattern=[[-1, P]], channel_multiplier=1).then_inc(consts, 1)

            def spread(b, t, tiles=1):
                n, ts = NB * b + t, slice(t, t + tiles)
                gp.wait_ge(mv_done, n + tiles)
                gp.sem_inc(gp_passed)
                gp.tensor_scalar(rstd[:, ts], mv[:, ts, 1], EPS, None, ALU.add).then_inc(ln_part, tiles)
                gp.tensor_scalar(negmean[:, ts], mv[:, ts, 0], -1.0, None, ALU.mult).then_inc(ln_part, tiles)
                gp.wait_ge(ln_part, 3 * n + 2 * tiles)
                gp.tensor_tensor(rstd[:, ts], rstd[:, ts], minus_half[:].to_broadcast([P, tiles]),
                                 ALU.pow).then_inc(ln_part, tiles)

            def normalise(b, t):
                r = t % XLN
                if some(b):
                    gp.wait_ge(xln_in[r], 16 * (XLN_USES[r] * (2 * b - 1) + t // XLN + 1))
                gp.wait_ge(ln_part, 3 * (NB * b + (t + 1 if some(b) else t // 2 * 2 + 2)))
                gp.sem_inc(gp_passed)
                tile = x_tile(b, t)
                gp.tensor_scalar(tile, tile, negmean[:, t:t + 1], rstd[:, t:t + 1],
                                 ALU.add, ALU.mult).then_inc(ln_done, 1)

            def split_v(b, j):
                gp.wait_ge(v_hi, NB * b + j + 1)
                v3 = vs[:, j, :, :].bitcast(F32)
                gp.tensor_tensor(vs[:, j, :, HD:], proj[:, j % 2, :].rearrange("p (h d) -> p h d", h=H),
                                 v3[:, :, :HD], ALU.subtract).then_inc(v_ready, 1)

            def low_k(b, p, k):
                n = 2 * (PAIRS * b + p) + k // 2
                cols = slice(k // 2 * HALF, (k // 2 + 1) * HALF)
                gp.wait_ge(qk_high, 4 * (PAIRS * b + p) * 2 + 2 * k + 2)
                for second in range(2):
                    _, hi_lo = qk_buffers(p, second)
                    rows = slice(HD * second, HD * second + HD)
                    gp.tensor_tensor(hi_lo[rows, 1, cols], proj[rows, k % 2, :],
                                     hi_lo[rows, 0, cols].bitcast(F32), ALU.subtract).then_inc(k_low, 1)
                    gp.wait_ge(k_low, 2 * n + 1 + second)
                gp.sem_inc(gp_passed)

            def finish(b, g):
                n, p = GROUPS * b + g, (g // 4) % 2
                y = yparts[:, :, 0]
                gp.wait_ge(y_copied, n + 1)
                gp.tensor_tensor(y, y, yparts[:, :, 1], ALU.add).then_inc(y_summed, 1)
                gp.wait_ge(inverted, n + 1)
                gp.wait_ge(y_summed, n + 1)
                gp.tensor_tensor(y, y, rinv[:, g % 2, :].unsqueeze(2).to_broadcast([P, GB, HD]),
                                 ALU.mult).then_inc(y_scaled, 1)
                gp.wait_ge(y_scaled, n + 1)
                if g % 4 == 0:
                    gp.wait_ge(xres_in[p], 16 * (2 * b + (g // 8) + 1))
                cols = HD * ((g // 2) % 2)
                dst = xres[:, p, GB * (g % 2):GB * (g % 2) + GB, cols:cols + HD]
                gp.tensor_tensor(dst, dst, y, ALU.add).then_inc(y_added, 1)

            for t in range(0, NB, 2):
                spread(0, t, 2)
                normalise(0, t)
                normalise(0, t + 1)
            for n in range(2 * (PAIRS - 1)):
                w, r = 1 - n // (PAIRS - 1), n % (PAIRS - 1)
                gp.wait_ge(w_hi, 2 + n + 1)
                parts = wqk_stage[:, r, w]
                gp.tensor_tensor(parts[:, :, 1, :], stage[:, w, :, (r + 1) * P:(r + 2) * P],
                                 parts[:, :, 0, :].bitcast(F32), ALU.subtract).then_inc(wqk_split, 1)
            for k in (0, 2):
                low_k(0, 0, k)
            for j in range(V_EARLY - 1):
                split_v(0, j)

            def body(b, first=False, last=False):
                for u in range(UNITS):
                    if u in STATS_AT and not last:
                        spread(b + 1, STATS_AT[u])
                    if u in NORM_AT and not last:
                        normalise(b + 1, NORM_AT[u])
                    if u in V_SPLIT_AT and not (last and u > V_FROM):
                        nxt, j = V_SPLIT_AT[u]
                        split_v(b + nxt, j)
                    v = u - HIGH_AFTER[1]
                    if v in QK_AT and QK_AT[v][1] % 2 == 0 and not (last and QK_AT[v][0] == PAIRS - 1):
                        low_k(b, QK_AT[v][0] + 1, QK_AT[v][1])
                    if u % NB == LAG and not (first and u == LAG):
                        if u == LAG:
                            finish(b - 1, GROUPS - 1)
                        else:
                            finish(b, u // NB - 1)

            body(0, first=True)
            with gp.Fori(1, B - 1) as b:
                body(b)
            body(B - 1, last=True)
            finish(B - 1, GROUPS - 1)

        @block.tensor
        def _(pe):
            def turn_h(b, t, free=None, bank=misc):
                pe.wait_ge(ln_done, NB * b + t + 1)
                if free:
                    pe.wait_ge(*free)
                for c in range(C):
                    mm = pe.transpose(bank[:, c * P:(c + 1) * P], x_tile(b, t)[:, c * P:(c + 1) * P], ident[:])
                mm.then_inc(h_turned, 1)

            def project_qk(b, p, k, part, free=None, bank=misc[:]):
                w, half = 1 - k % 2, k // 2
                pair = PAIRS * b + p
                cols = slice(half * HALF, (half + 1) * HALF)
                if part == 0:
                    pe.wait_ge(h_lo, NB * (b + p // PAIRS) + GB * (half + 1))
                    if some(pair):
                        pe.wait_ge(wqk_in, 16 * pair)
                    else:
                        pe.wait_ge(w0_split, 2 if k else 1)
                    if free:
                        pe.wait_ge(*free)
                parts = [(c, wl, hl) for c in range(C) for wl, hl in ((0, 0), (0, 1), (1, 0))]
                count = len(parts) // 2
                for n in range(part * count, (part + 1) * count):
                    c, wl, hl = parts[n]
                    mm = pe.matmul(bank, wqk[:, w, c, wl, :], hT[:, hl, c, cols],
                                   start=n == 0, stop=n == len(parts) - 1)
                if part == 1:
                    mm.then_inc(qk_mm, 1)

            def project_v(b, j, free, bank=misc[:]):
                pe.wait_ge(h_lo, NB * (b + 1))
                pe.wait_ge(*free)
                if isinstance(b, int) and b == 0:
                    pe.wait_ge(wv_split, 1)
                parts = [(c, wl, hl) for c in range(C) for wl, hl in ((0, 0), (1, 0), (0, 1))]
                for n, (c, wl, hl) in enumerate(parts):
                    mm = pe.matmul(bank, hT[:, hl, c, j * P:(j + 1) * P], wv[:, wl, c, :],
                                   start=n == 0, stop=n == len(parts) - 1)
                mm.then_inc(v_mm, 1)

            def score(b, s):
                n = SBLOCKS * b + s
                q, k = qk_buffers(s // 16, (s // 8) % 2)
                i = s % NB
                pair = PAIRS * b + s // 16
                pe.wait_ge(q_low, 4 * pair + 3 + (s // 8) % 2)
                pe.wait_ge(k_copied, 64 * (pair + 1))
                if some(n - 1):
                    pe.wait_ge(exped, n - 1)
                for half in range(2):
                    cols = slice(half * HALF, (half + 1) * HALF)
                    dst = S[:, s % 2, cols]
                    pe.matmul(dst, q[:, i * P:(i + 1) * P], k[:, 0, cols], start=True, stop=False)
                    mm = pe.matmul(dst, q[:, i * P:(i + 1) * P], k[:, 1, cols], start=False, stop=True)
                mm.then_inc(scored, 1)

            def turn_probs(b, u):
                n, g, j = UNITS * b + u, u // NB, u % NB
                if j == 0:
                    pe.wait_ge(exped, GB * (GROUPS * b + g + 1))
                if some(n - 1):
                    pe.wait_ge(p_lo, n - 1)
                for i in range(GB):
                    mm = pe.transpose(T[:, u % 2, i * P:(i + 1) * P],
                                      probs[:, (GB * g + i) % RING, j * P:(j + 1) * P], ident[:])
                mm.then_inc(turned, 1)

            def contract(b, u):
                n, g, j, head = UNITS * b + u, u // NB, u % NB, u // (2 * NB)
                if g == 0:
                    pe.wait_ge(v_ready, NB * b + j + 1)
                if j == 0 and some(GROUPS * b + g):
                    pe.wait_ge(o_copied, GROUPS * b + g)
                pe.wait_ge(p_lo, n + 1)
                for part in range(2):
                    mm = pe.matmul(O[:], vs[:, j, head, :], pT[:, u % PT, part, :],
                                   start=(j == 0 and part == 0), stop=(j == NB - 1 and part == 1))
                mm.then_inc(contracted, 1)

            def turn_out(b, g, free):
                pe.wait_ge(o_copied, GROUPS * b + g + 1)
                pe.wait_ge(*free)
                for i in range(GB):
                    mm = pe.transpose(misc[:, i * P:(i + 1) * P], oT[:, i * P:(i + 1) * P], ident[:])
                mm.then_inc(o_turned, 1)

            def score_ahead(b, u, last):
                s = u // 2 + LEAD
                if u % 2 == 0 and s < SBLOCKS:
                    score(b, s)
                if u % 2 == 0 and s >= SBLOCKS and not last:
                    score(b + 1, s - SBLOCKS)

            def fill(b, u, last):
                if u in V_AT and not (last and u >= V_FROM):
                    nxt, j = V_AT[u]
                    project_v(b + nxt, j, before(b, u, False, last))
                if u in QK_START and not (last and QK_START[u][0] == PAIRS - 1):
                    p, k = QK_START[u]
                    project_qk(b, p + 1, k, 0, before(b, u, False, last))
                if u in QK_AT and not (last and QK_AT[u][0] == PAIRS - 1):
                    p, k = QK_AT[u]
                    project_qk(b, p + 1, k, 1)
                if u in HT_AT and not last:
                    turn_h(b + 1, HT_AT[u], before(b, u, False, last))

            pe.wait_ge(consts, 1)
            for t in range(NB):
                turn_h(0, t, (h_lo, t - 3) if t > 3 else None, h_banks[t % 4])
            for k in range(4):
                for part in range(2):
                    project_qk(0, 0, k, part, None, mm_banks[k])
            for j in range(V_EARLY):
                project_v(0, j, (v_biased, j - 3) if j > 3 else (qk_evac, j + 1), mm_banks[j % 4])
            for s in range(LEAD):
                score(0, s)

            def body(b, first=False, last=False):
                for u in range(UNITS):
                    if u % NB == LAG:
                        turn_probs(b, u)
                        score_ahead(b, u, last)
                        contract(b, u - LAG)
                        if u == LAG and not first:
                            turn_out(b - 1, GROUPS - 1, before(b, u, True, last))
                        if u > LAG:
                            turn_out(b, u // NB - 1, before(b, u, True, last))
                        continue
                    if u >= LAG:
                        contract(b, u - LAG)
                    elif not first:
                        contract(b - 1, UNITS - LAG + u)
                    turn_probs(b, u)
                    score_ahead(b, u, last)
                    fill(b, u, last)

            body(0, first=True)
            with pe.Fori(1, B - 1) as b:
                body(b)
            body(B - 1, last=True)
            for u in range(UNITS - LAG, UNITS):
                contract(B - 1, u)
            turn_out(B - 1, GROUPS - 1, (y_copied, GROUPS * B - 1))

        @block.scalar
        def _(act):
            def copy_out(b, g):
                n = GROUPS * b + g
                act.wait_ge(contracted, NB * (n + 1))
                if some(n):
                    act.wait_ge(o_turned, n)
                act.copy(oT[:], O[:]).then_inc(o_copied, 1)

            def copy_y(b, g):
                n = GROUPS * b + g
                act.wait_ge(o_turned, n + 1)
                if some(n):
                    act.wait_ge(y_added, n)
                act.copy(yparts[:].rearrange("p i l d -> p (i l d)"), misc[:]).then_inc(y_copied, 1)

            def probs_hi(b, u):
                n = UNITS * b + u
                act.wait_ge(turned, n + 1)
                used = n + 1 - (PT if u >= PT - 1 else PT - 1)
                if some(used):
                    act.wait_ge(contracted, used)
                act.copy(pT[:, u % PT, 0, :], T[:, u % 2, :]).then_inc(p_hi, 1)

            def exponential(b, s):
                n = SBLOCKS * b + s
                free = NB * (GROUPS * b + s // GB - 1)
                if some(free):
                    act.wait_ge(turned, free)
                act.wait_ge(shifted, n + 1)
                act.activation(probs[:, s % RING, :], S[:, s % 2, :], ACT.Exp,
                               bias=negmax[:, s % RING:s % RING + 1], scale=-1.0,
                               accum_out=rowsum[:, s % (2 * RING):s % (2 * RING) + 1]).then_inc(exped, 1)

            def evacuate_qk(b, p, k, bank=misc[:]):
                w, pair = 1 - k % 2, PAIRS * b + p
                act.wait_ge(qk_mm, 4 * pair + k + 1)
                if p == 1 and k < 2:
                    act.wait_ge(v_ready, NB * (b + 1) - 1 + k)
                if some(2 * pair + k // 2):
                    act.wait_ge(q_low if k % 2 else k_low, 2 * (2 * pair + k // 2))
                act.activation(proj[:, k % 2], bank, ACT.Identity, bias=bqk[:, w, p % PAIRS:p % PAIRS + 1],
                               scale=-SCALE if w == 0 else 1.0).then_inc(qk_evac, 1)

            def high(b, p, k, second):
                cols = slice(k // 2 * HALF, (k // 2 + 1) * HALF)
                q, hi_lo = qk_buffers(p, second)
                rows = slice(HD * second, HD * second + HD)
                if not second:
                    act.wait_ge(qk_evac, 4 * (PAIRS * b + p) + k + 1)
                act.copy(q[rows, cols] if k % 2 else hi_lo[rows, 0, cols],
                         proj[rows, k % 2, :]).then_inc(qk_high, 1)

            def h_high(b, t, bank=misc[:]):
                act.wait_ge(h_turned, NB * b + t + 1)
                act.activation(hT[:, 0, :, t * P:(t + 1) * P], bank.rearrange("p (c n) -> p c n", c=C),
                               ACT.Relu).then_inc(h_hi, 1)

            def v_high(b, j):
                act.wait_ge(v_biased, NB * b + j + 1)
                used = UNITS * (b - 1) + UNITS - NB + j + 1
                if some(used):
                    act.wait_ge(contracted, used)
                elif j > 1:
                    act.wait_ge(wqk_stored[j // 2], 16)
                act.copy(vs[:, j, :, :HD], proj[:, j % 2, :].rearrange("p (h d) -> p h d", h=H)).then_inc(v_hi, 1)

            def w_high(w, r):
                if r == 0:
                    act.wait_ge(w_in[w], 16)
                parts = wqk[:, w] if r == 0 else wqk_stage[:, r - 1, w]
                act.copy(parts[:, :, 0, :], stage[:, w, :, r * P:(r + 1) * P]).then_inc(w_hi, 1)

            for t in range(GB):
                h_high(0, t, h_banks[t % 4])
            for w in (1, 0):
                w_high(w, 0)
            for t in range(GB, NB):
                h_high(0, t, h_banks[t % 4])
            for w in (1, 0):
                for r in range(1, PAIRS):
                    w_high(w, r)
            act.wait_ge(w_in[2], 16)
            act.copy(wv[:, 0], stage[:, 2]).then_inc(wv_hi, 1)
            act.wait_ge(bias_made, 1)
            for k in range(4):
                evacuate_qk(0, 0, k, mm_banks[k])
                high(0, 0, k, 0)
                high(0, 0, k, 1)
            for j in range(V_EARLY - 1):
                v_high(0, j)
            for s in range(LEAD - 1):
                exponential(0, s)

            def body(b, first=False, last=False):
                for u in range(UNITS):
                    if u == 1 and not first:
                        copy_out(b - 1, GROUPS - 1)
                    if u > 1 and u % NB == 1:
                        copy_out(b, u // NB - 1)
                    probs_hi(b, u)
                    s = u // 2 + LEAD - 1
                    if u % 2 == 0 and s < SBLOCKS:
                        exponential(b, s)
                    if u % 2 == 0 and s >= SBLOCKS and not last:
                        exponential(b + 1, s - SBLOCKS)
                    if u == LAG and not first:
                        copy_y(b - 1, GROUPS - 1)
                    if u > LAG and u % NB == LAG:
                        copy_y(b, u // NB - 1)
                    if u in V_SPLIT_AT and not (last and u > V_FROM):
                        nxt, j = V_SPLIT_AT[u]
                        v_high(b + nxt, j)
                    if u in QK_AT and not (last and QK_AT[u][0] == PAIRS - 1):
                        evacuate_qk(b, QK_AT[u][0] + 1, QK_AT[u][1])
                    for second in range(2):
                        v = u - HIGH_AFTER[second]
                        if v in QK_AT and not (last and QK_AT[v][0] == PAIRS - 1):
                            high(b, QK_AT[v][0] + 1, QK_AT[v][1], second)
                    if u in HT_AT and not last:
                        h_high(b + 1, HT_AT[u])

            body(0, first=True)
            with act.Fori(1, B - 1) as b:
                body(b)
            body(B - 1, last=True)
            copy_out(B - 1, GROUPS - 1)
            copy_y(B - 1, GROUPS - 1)

        @block.vector
        def _(dve):
            def stats(b, t):
                r, n = t % XLN, NB * b + t
                if some(b):
                    dve.wait_ge(xln_in[r], 16 * (XLN_USES[r] * 2 * (b - 1) + t // XLN + 1))
                else:
                    dve.wait_ge(x0_in[t // 2], 16)
                dve.bn_stats(bn[:, r, :], x_tile(b, t)).then_inc(bn_done, 1)
                dve.wait_ge(bn_done, n + 1)
                dve.sem_inc(dve_passed)
                dve.bn_aggr(mv[:, t, :], bn[:, r, :]).then_inc(mv_done, 1)

            def h_low(b, t, bank=misc[:]):
                dve.wait_ge(h_hi, NB * b + t + 1)
                cols = slice(t * P, (t + 1) * P)
                dve.scalar_tensor_tensor(hT[:, 1, :, cols], bank.rearrange("p (c n) -> p c n", c=C), 0.0,
                                         hT[:, 0, :, cols].bitcast(F32), ALU.max, ALU.subtract).then_inc(h_lo, 1)

            def low_q(b, p, k, second):
                n = 4 * (PAIRS * b + p) + k
                cols = slice(k // 2 * HALF, (k // 2 + 1) * HALF)
                q, _ = qk_buffers(p, second)
                at = HD * second
                dve.wait_ge(qk_high, 2 * n + 1 + second)
                dve.tensor_tensor(q[HD - at:2 * HD - at, cols], proj[at:at + HD, k % 2, :],
                                  q[at:at + HD, cols].bitcast(F32), ALU.subtract).then_inc(q_low, 1)

            def bias_v(b, j, bank=misc[:]):
                n = NB * b + j
                dve.wait_ge(v_mm, n + 1)
                if j < 2:
                    dve.wait_ge((k_low, q_low)[j], 4 * (PAIRS * b + 1))
                else:
                    dve.wait_ge(v_ready, n - 1)
                dve.tensor_tensor(proj[:, j % 2, :], bank, bv_all[:], ALU.add).then_inc(v_biased, 1)

            def shift(b, s):
                n = SBLOCKS * b + s
                dve.wait_ge(scored, n + 1)
                dve.sem_inc(dve_passed)
                dve.tensor_tensor_reduce(S[:, s % 2, :], S[:, s % 2, :], mask[:, s % NB, :], 1.0,
                                         3.0e38, ALU.add, ALU.min,
                                         negmax[:, s % RING:s % RING + 1]).then_inc(shifted, 1)

            def probs_low(b, u):
                dve.wait_ge(p_hi, UNITS * b + u + 1)
                dve.tensor_tensor(pT[:, u % PT, 1, :], T[:, u % 2, :], pT[:, u % PT, 0, :].bitcast(F32),
                                  ALU.subtract).then_inc(p_lo, 1)

            def invert(b, g):
                n, r = GROUPS * b + g, g % 2
                if some(n - 1):
                    dve.wait_ge(y_added, n - 1)
                dve.wait_ge(exped, GB * (n + 1))
                at = GB * g % (2 * RING)
                dve.reciprocal(rinv[:, r, :], rowsum[:, at:at + GB]).then_inc(inverted, 1)

            dve.wait_ge(b_in, 48)
            dve.tensor_scalar(bqk[:, 0, :], bqk[:, 0, :], -SCALE, None, ALU.mult).then_inc(bias_made, 1)
            for t in range(NB):
                stats(0, t)

            def w_low(n, w):
                dve.wait_ge(w_hi, n)
                dve.tensor_tensor(wqk[:, w, :, 1, :], stage[:, w, :, 0:P], wqk[:, w, :, 0, :].bitcast(F32),
                                  ALU.subtract).then_inc(w0_split, 1)

            for t in range(GB):
                h_low(0, t, h_banks[t % 4])
            w_low(1, 1)
            w_low(2, 0)
            for t in range(GB, NB):
                h_low(0, t, h_banks[t % 4])
            dve.wait_ge(wv_hi, 1)
            dve.tensor_tensor(wv[:, 1], stage[:, 2], wv[:, 0].bitcast(F32), ALU.subtract).then_inc(wv_split, 1)
            for k in (1, 3):
                low_q(0, 0, k, 0)
                low_q(0, 0, k, 1)

            def make_mask(i):
                dve.wait_ge(adj_in[i], 16)
                dve.tensor_scalar(mask[:, 2 * i:2 * i + 2, :], probs[:, 2 * i:2 * i + 2, :], 0.0, MASKED,
                                  ALU.is_equal, ALU.mult).then_inc(mask_made, 1)

            masks = [3, 1, 0, 2]
            for j in range(V_EARLY):
                bias_v(0, j, mm_banks[j % 4])
                if j in (1, 2, 3, 4):
                    make_mask(masks[j - 1])
            dve.wait_ge(mask_made, 4)
            for s in range(LEAD):
                shift(0, s)

            def body(b, first=False, last=False):
                for u in range(UNITS):
                    if u == LAG and not first:
                        invert(b - 1, GROUPS - 1)
                    if u > LAG and u % NB == LAG:
                        invert(b, u // NB - 1)
                    if u - 1 in HT_AT and not last:
                        h_low(b + 1, HT_AT[u - 1])
                    probs_low(b, u)
                    s = u // 2 + LEAD
                    if u % 2 == 0 and s < SBLOCKS:
                        shift(b, s)
                    if u % 2 == 0 and s >= SBLOCKS and not last:
                        shift(b + 1, s - SBLOCKS)
                    if u in V_AT and not (last and u >= V_FROM):
                        bias_v(b + V_AT[u][0], V_AT[u][1])
                    for second in range(2):
                        v = u - LOW_AFTER[second]
                        if v in QK_AT and QK_AT[v][1] % 2 and not (last and QK_AT[v][0] == PAIRS - 1):
                            low_q(b, QK_AT[v][0] + 1, QK_AT[v][1], second)
                    if u in STATS_AT and not last:
                        stats(b + 1, STATS_AT[u])

            body(0, first=True)
            with dve.Fori(1, B - 1) as b:
                body(b)
            body(B - 1, last=True)
            invert(B - 1, GROUPS - 1)


_INS = ["x", "adj", "L0_gnn_Wq", "L0_gnn_bq", "L0_gnn_Wk", "L0_gnn_bk", "L0_gnn_Wv", "L0_gnn_bv"]


def kernel(**inputs):
    import concourse.bacc as bacc
    from concourse.bass_utils import run_bass_kernel_spmd

    nc = bacc.Bacc("TRN2", target_bir_lowering=False, num_devices=1)
    arrays, args = {}, []
    for name in _INS:
        a = np.ascontiguousarray(inputs[name])
        arrays[f"in_{name}"] = a
        args.append(nc.dram_tensor(f"in_{name}", a.shape, mybir.dt.from_np(a.dtype), kind="ExternalInput").ap())
    args.append(nc.dram_tensor("out_0", (B, N, D), F32, kind="ExternalOutput").ap())
    adj_preln_kernel(nc, *args)
    r = run_bass_kernel_spmd(nc, [arrays], core_ids=[0])
    return r.results[0]["out_0"]
```
